# Optimizing a Trainium2 kernel written in Bass

```python
import numpy as np
import jax
import jax.numpy as jnp

def _softmax(x, axis=-1):
    return jax.nn.softmax(x, axis=axis)
def _gelu(x):
    return jax.nn.gelu(x, approximate=True)
def _silu(x):
    return jax.nn.silu(x)
def _sigmoid(x):
    return jax.nn.sigmoid(x)
def _layernorm(x, axis=-1, eps=1e-5):
    m = jnp.mean(x, axis=axis, keepdims=True)
    v = jnp.var(x, axis=axis, keepdims=True)
    return (x - m) / jnp.sqrt(v + eps)
def _scatter_add(tgt, idx, src, axis=0):
    return tgt.at[idx].add(src)
def _segment_sum(src, seg, n):
    return jax.ops.segment_sum(src, seg, n)

kernel_name = 'mk_conv_preact_d2_conv_nchw384_2502b5'

def setup_inputs(seed: int = 0):
    np.random.seed(seed)
    _w = jnp.asarray
    def _rec_inputs():
        import jax
        import jax.numpy as jnp
        _gk = jax.random.key(seed)
        x = -0.000224 + 1 * jax.random.normal(jax.random.fold_in(_gk, 1), (2, 384, 96, 96), jnp.float32)
        return x
    x = _rec_inputs()
    def _L0_conv_setup():
        import jax, jax.numpy as jnp
        import numpy as np
        DIM = 384
        N_HEADS = 12
        HEAD_DIM = DIM // N_HEADS
        L_HEADS = int(N_HEADS * 0.5)
        H_HEADS = N_HEADS - L_HEADS
        L_DIM = L_HEADS * HEAD_DIM
        H_DIM = H_HEADS * HEAD_DIM
        WS = 2
        SCALE = HEAD_DIM ** (-0.5)
        B, H, W = (2, 96, 96)

        def _hifi(x, Wh_qkv, Wh_proj, bh_proj):
            Bx, Hx, Wx, C = x.shape
            hg, wg = (Hx // WS, Wx // WS)
            G, n = (hg * wg, WS * WS)
            xw = x.reshape(Bx, hg, WS, wg, WS, C).transpose(0, 1, 3, 2, 4, 5).reshape(Bx, G, n, C)
            qkv = (xw @ Wh_qkv).reshape(Bx, G, n, 3, H_HEADS, HEAD_DIM)
            qkv = qkv.transpose(3, 0, 1, 4, 2, 5)
            q, k, v = (qkv[0], qkv[1], qkv[2])
            attn = jnp.einsum('bghnd,bghmd->bghnm', q, k) * SCALE
            attn = jax.nn.softmax(attn, axis=-1)
            out = jnp.einsum('bghnm,bghmd->bghnd', attn, v)
            out = out.transpose(0, 1, 3, 2, 4).reshape(Bx, hg, wg, WS, WS, H_DIM)
            out = out.transpose(0, 1, 3, 2, 4, 5).reshape(Bx, Hx, Wx, H_DIM)
            return out @ Wh_proj + bh_proj

        def _lofi(x, Wl_q, Wl_kv, Wl_proj, bl_proj):
            Bx, Hx, Wx, C = x.shape
            N = Hx * Wx
            q = (x.reshape(Bx, N, C) @ Wl_q).reshape(Bx, N, L_HEADS, HEAD_DIM).transpose(0, 2, 1, 3)
            xp = x.reshape(Bx, Hx // WS, WS, Wx // WS, WS, C).mean(axis=(2, 4))
            M = Hx // WS * (Wx // WS)
            kv = (xp.reshape(Bx, M, C) @ Wl_kv).reshape(Bx, M, 2, L_HEADS, HEAD_DIM)
            kv = kv.transpose(2, 0, 3, 1, 4)
            k, v = (kv[0], kv[1])
            attn = jnp.einsum('bhnd,bhmd->bhnm', q, k) * SCALE
            attn = jax.nn.softmax(attn, axis=-1)
            out = jnp.einsum('bhnm,bhmd->bhnd', attn, v)
            out = out.transpose(0, 2, 1, 3).reshape(Bx, Hx, Wx, L_DIM)
            return out @ Wl_proj + bl_proj
        key = jax.random.key(seed)
        ks = jax.random.split(key, 8)
        s = 0.02
        return {'x': jax.random.normal(ks[0], (B, DIM, H, W), jnp.float32), 'Wh_qkv': jax.random.normal(ks[1], (DIM, H_DIM * 3), jnp.float32) * s, 'Wh_proj': jax.random.normal(ks[2], (H_DIM, H_DIM), jnp.float32) * s, 'bh_proj': jnp.zeros((H_DIM,), jnp.float32), 'Wl_q': jax.random.normal(ks[3], (DIM, L_DIM), jnp.float32) * s, 'Wl_kv': jax.random.normal(ks[4], (DIM, L_DIM * 2), jnp.float32) * s, 'Wl_proj': jax.random.normal(ks[5], (L_DIM, L_DIM), jnp.float32) * s, 'bl_proj': jnp.zeros((L_DIM,), jnp.float32)}
    _L0_conv_all = _L0_conv_setup()
    _L0_conv_in = {k: v for k, v in _L0_conv_all.items() if k in ('Wh_qkv', 'Wh_proj', 'bh_proj', 'Wl_q', 'Wl_kv', 'Wl_proj', 'bl_proj', )}
    del _L0_conv_all

    def _L1_conv_setup():
        import jax, jax.numpy as jnp
        from jax import lax
        import numpy as np
        H, W = (64, 64)
        K = 5
        SIGMA = 0.5
        CHAN_PER_POS = 8
        INIT_STRIDE = 16
        BATCH = 32

        def _num_offsets(h, w, s):
            ny = (h - s) // s * 2 + 1
            nx = (w - s) // s * 2 + 1
            return (ny, nx, ny * nx - 1)

        def _displace(x, off_int):
            _, _, _, h, w = x.shape

            def shift_one(xp, dxy):
                dx, dy = (dxy[0], dxy[1])
                ys = jnp.arange(h) - dy
                xs = jnp.arange(w) - dx
                ym = (ys >= 0) & (ys < h)
                xm = (xs >= 0) & (xs < w)
                ysc = jnp.clip(ys, 0, h - 1)
                xsc = jnp.clip(xs, 0, w - 1)
                out = xp[:, :, ysc][:, :, :, xsc]
                return out * (ym[:, None] & xm[None, :]).astype(xp.dtype)
            return jax.vmap(shift_one, in_axes=(1, 0), out_axes=1)(x, off_int)
        key = jax.random.key(seed)
        k1, k2 = jax.random.split(key)
        ny, nx, npos = _num_offsets(H, W, INIT_STRIDE)
        C = npos * CHAN_PER_POS
        x = jax.random.normal(k1, (BATCH, C, H, W), dtype=jnp.float32)
        offs = []
        for ih in range(-(ny // 2), ny // 2 + 1):
            for iw in range(-(nx // 2), nx // 2 + 1):
                if ih == 0 and iw == 0:
                    continue
                offs.append([iw * INIT_STRIDE, ih * INIT_STRIDE])
        offset = jnp.asarray(np.array(offs, dtype=np.float32))
        offset = offset + jax.random.uniform(k2, offset.shape, dtype=jnp.float32, minval=-0.4, maxval=0.4)
        return {'x': x, 'offset': offset}
    _L1_conv_all = _L1_conv_setup()
    _L1_conv_in = {k: v for k, v in _L1_conv_all.items() if k in ('offset', )}
    del _L1_conv_all

    return {
        "x": x,
        "L0_conv_Wh_qkv": _L0_conv_in["Wh_qkv"],
        "L0_conv_Wh_proj": _L0_conv_in["Wh_proj"],
        "L0_conv_bh_proj": _L0_conv_in["bh_proj"],
        "L0_conv_Wl_q": _L0_conv_in["Wl_q"],
        "L0_conv_Wl_kv": _L0_conv_in["Wl_kv"],
        "L0_conv_Wl_proj": _L0_conv_in["Wl_proj"],
        "L0_conv_bl_proj": _L0_conv_in["bl_proj"],
        "L1_conv_offset": _L1_conv_in["offset"],
    }

def reference(x, L0_conv_Wh_qkv, L0_conv_Wh_proj, L0_conv_bh_proj, L0_conv_Wl_q, L0_conv_Wl_kv, L0_conv_Wl_proj, L0_conv_bl_proj, L1_conv_offset):
    import jax
    import jax.numpy as jnp
    def _L0_conv_ref(x, Wh_qkv, Wh_proj, bh_proj, Wl_q, Wl_kv, Wl_proj, bl_proj):
        import jax, jax.numpy as jnp
        import numpy as np
        DIM = 384
        N_HEADS = 12
        HEAD_DIM = DIM // N_HEADS
        L_HEADS = int(N_HEADS * 0.5)
        H_HEADS = N_HEADS - L_HEADS
        L_DIM = L_HEADS * HEAD_DIM
        H_DIM = H_HEADS * HEAD_DIM
        WS = 2
        SCALE = HEAD_DIM ** (-0.5)
        B, H, W = (2, 96, 96)

        def _hifi(x, Wh_qkv, Wh_proj, bh_proj):
            Bx, Hx, Wx, C = x.shape
            hg, wg = (Hx // WS, Wx // WS)
            G, n = (hg * wg, WS * WS)
            xw = x.reshape(Bx, hg, WS, wg, WS, C).transpose(0, 1, 3, 2, 4, 5).reshape(Bx, G, n, C)
            qkv = (xw @ Wh_qkv).reshape(Bx, G, n, 3, H_HEADS, HEAD_DIM)
            qkv = qkv.transpose(3, 0, 1, 4, 2, 5)
            q, k, v = (qkv[0], qkv[1], qkv[2])
            attn = jnp.einsum('bghnd,bghmd->bghnm', q, k) * SCALE
            attn = jax.nn.softmax(attn, axis=-1)
            out = jnp.einsum('bghnm,bghmd->bghnd', attn, v)
            out = out.transpose(0, 1, 3, 2, 4).reshape(Bx, hg, wg, WS, WS, H_DIM)
            out = out.transpose(0, 1, 3, 2, 4, 5).reshape(Bx, Hx, Wx, H_DIM)
            return out @ Wh_proj + bh_proj

        def _lofi(x, Wl_q, Wl_kv, Wl_proj, bl_proj):
            Bx, Hx, Wx, C = x.shape
            N = Hx * Wx
            q = (x.reshape(Bx, N, C) @ Wl_q).reshape(Bx, N, L_HEADS, HEAD_DIM).transpose(0, 2, 1, 3)
            xp = x.reshape(Bx, Hx // WS, WS, Wx // WS, WS, C).mean(axis=(2, 4))
            M = Hx // WS * (Wx // WS)
            kv = (xp.reshape(Bx, M, C) @ Wl_kv).reshape(Bx, M, 2, L_HEADS, HEAD_DIM)
            kv = kv.transpose(2, 0, 3, 1, 4)
            k, v = (kv[0], kv[1])
            attn = jnp.einsum('bhnd,bhmd->bhnm', q, k) * SCALE
            attn = jax.nn.softmax(attn, axis=-1)
            out = jnp.einsum('bhnm,bhmd->bhnd', attn, v)
            out = out.transpose(0, 2, 1, 3).reshape(Bx, Hx, Wx, L_DIM)
            return out @ Wl_proj + bl_proj
        Bx, C, Hx, Wx = x.shape
        xc = x.transpose(0, 2, 3, 1)
        hi = _hifi(xc, Wh_qkv, Wh_proj, bh_proj)
        lo = _lofi(xc, Wl_q, Wl_kv, Wl_proj, bl_proj)
        out = jnp.concatenate((hi, lo), axis=-1).reshape(Bx, Hx * Wx, C)
        return out.transpose(0, 2, 1).reshape(Bx, C, Hx, Wx)

    def _L1_conv_ref(x, offset):
        import jax, jax.numpy as jnp
        from jax import lax
        import numpy as np
        H, W = (64, 64)
        K = 5
        SIGMA = 0.5
        CHAN_PER_POS = 8
        INIT_STRIDE = 16
        BATCH = 32

        def _num_offsets(h, w, s):
            ny = (h - s) // s * 2 + 1
            nx = (w - s) // s * 2 + 1
            return (ny, nx, ny * nx - 1)

        def _displace(x, off_int):
            _, _, _, h, w = x.shape

            def shift_one(xp, dxy):
                dx, dy = (dxy[0], dxy[1])
                ys = jnp.arange(h) - dy
                xs = jnp.arange(w) - dx
                ym = (ys >= 0) & (ys < h)
                xm = (xs >= 0) & (xs < w)
                ysc = jnp.clip(ys, 0, h - 1)
                xsc = jnp.clip(xs, 0, w - 1)
                out = xp[:, :, ysc][:, :, :, xsc]
                return out * (ym[:, None] & xm[None, :]).astype(xp.dtype)
            return jax.vmap(shift_one, in_axes=(1, 0), out_axes=1)(x, off_int)
        B, C, h, w = x.shape
        P = offset.shape[0]
        cpp = C // P
        off_round = jnp.round(offset)
        off_int = off_round.astype(jnp.int32)
        disp = _displace(x.reshape(B, P, cpp, h, w), off_int).reshape(B, C, h, w)
        sub = offset - lax.stop_gradient(off_round)
        c = K // 2
        jj, ii = jnp.meshgrid(jnp.arange(K, dtype=jnp.float32) - c, jnp.arange(K, dtype=jnp.float32) - c, indexing='xy')
        field = jnp.stack([jj, ii], axis=-1)
        d = field[None] + sub[:, None, None, :]
        kernel = jnp.exp(-jnp.sum(d * d, axis=-1) / (2.0 * SIGMA ** 2))
        kernel = kernel / jnp.sum(kernel, axis=(1, 2), keepdims=True)
        kw = jnp.repeat(kernel, cpp, axis=0)[:, None]
        out = lax.conv_general_dilated(disp, kw, window_strides=(1, 1), padding=[(c, c), (c, c)], feature_group_count=C, dimension_numbers=('NCHW', 'OIHW', 'NCHW'))
        return out

    def _gn(v, G=32, eps=1e-5):
        B_, C_, H_, W_ = v.shape
        g = v.reshape(B_, G, C_ // G, H_, W_)
        m = jnp.mean(g, axis=(2, 3, 4), keepdims=True)
        s = jnp.var(g, axis=(2, 3, 4), keepdims=True)
        return ((g - m) / jnp.sqrt(s + eps)).reshape(v.shape)

    def _ln_c(v, eps=1e-6):
        m = jnp.mean(v, axis=1, keepdims=True)
        s = jnp.var(v, axis=1, keepdims=True)
        return (v - m) / jnp.sqrt(s + eps)

    def _ln_t(v, eps=1e-5):
        m = jnp.mean(v, axis=-1, keepdims=True)
        s = jnp.var(v, axis=-1, keepdims=True)
        return (v - m) / jnp.sqrt(s + eps)

    def _to_tokens(v):
        B_, C_, H_, W_ = v.shape
        return v.reshape(B_, C_, H_ * W_).transpose(0, 2, 1)
    def _from_tokens(t, like):
        B_, C_, H_, W_ = like.shape
        return t.transpose(0, 2, 1).reshape(B_, C_, H_, W_)

    x = x + _L0_conv_ref(_gn(x), L0_conv_Wh_qkv, L0_conv_Wh_proj, L0_conv_bh_proj, L0_conv_Wl_q, L0_conv_Wl_kv, L0_conv_Wl_proj, L0_conv_bl_proj)
    x = x + _L1_conv_ref(_gn(x), L1_conv_offset)
    return x


_drawn_inputs = setup_inputs


def setup_inputs(seed=0):
    import zlib

    import numpy as np

    out = dict(_drawn_inputs(seed))
    spreads = {'L0_conv_bh_proj': (0.0, 0.1), 'L0_conv_bl_proj': (0.0, 0.1)}
    factors = {'L0_conv_Wl_q': 8.0, 'L0_conv_Wl_kv': 8.0, 'L0_conv_Wl_proj': 8.0}
    for name, (base, spread) in spreads.items():
        noise = np.random.default_rng([zlib.crc32(name.encode()), seed]).standard_normal(out[name].shape)
        drawn = base * np.exp(spread * noise) if base else spread * noise
        out[name] = jnp.asarray(drawn.astype(out[name].dtype))
    for name, factor in factors.items():
        out[name] = (out[name] * factor).astype(out[name].dtype)
    return out
```

```python
import concourse.bass as bass
from concourse import mybir
from contextlib import ExitStack


def group_scales(nc, x, to_groups, from_groups, mean_rstd):
    f32 = mybir.dt.float32
    ALU, ACT = mybir.AluOpType, mybir.ActivationFunctionType
    BATCH, C, PIX = x.shape[0], x.shape[1], x.shape[2]
    LANES, EPS, STAT = 128, 1e-5, 512
    CT = C // LANES
    NG = to_groups.shape[2]
    PIECE = PIX // 2
    LOADS = BATCH * CT * 2
    BUFS = 4
    PER = PIECE // STAT

    with ExitStack() as ctx:
        def sb(name, shape):
            return ctx.enter_context(nc.sbuf_tensor(name, shape, f32))

        def sem(name):
            return ctx.enter_context(nc.semaphore(name))

        pieces = sb("pieces", [LANES, BUFS, PIECE])
        stats = sb("gn_stats", [LANES, CT, BATCH, 2 * PER * 6])
        mean_sq = sb("mean_sq", [LANES, CT, BATCH, 2])
        square = sb("gn_square", [LANES, CT, BATCH])
        to_g = sb("to_g", [LANES, CT, NG])
        from_g = sb("from_g", [NG, C])
        group = sb("group", [NG, BATCH, 2])
        gsq = sb("gsq", [NG, BATCH])
        newton = sb("newton", [NG, BATCH])
        g_ps = ctx.enter_context(nc.psum_tensor("g_ps", [LANES, 512], f32))
        b_ps = ctx.enter_context(nc.psum_tensor("b_ps", [LANES, 512], f32))
        piece_in = [sem(f"piece_in{i}") for i in range(BUFS)]
        const_in, stat_done, step = sem("const_in"), sem("stat_done"), sem("gn_step")
        grouped, spread, rooted, summed = sem("grouped"), sem("spread"), sem("rooted"), sem("summed")
        block = ctx.enter_context(nc.Block())

        @block.sync
        def _(sp):
            sp.dma_start(to_g[:, :, :], to_groups).then_inc(const_in, 16)
            sp.dma_start(from_g[:, :], from_groups).then_inc(const_in, 16)
            for n in range(LOADS):
                b, ct, half = n // (2 * CT), n // 2 % CT, n % 2
                if n >= BUFS:
                    sp.wait_ge(stat_done, PER * (n - BUFS + 1))
                sp.dma_start(pieces[:, n % BUFS, :], x[b, ct * LANES:(ct + 1) * LANES, half * PIECE:(half + 1) * PIECE])\
                  .then_inc(piece_in[n % BUFS], 16)

        @block.vector
        def _(dve):
            count = [0]

            def link(ins):
                count[0] += 1
                ins.then_inc(step, 1)
                dve.wait_ge(step, count[0])

            for n in range(LOADS):
                b, ct, half = n // (2 * CT), n // 2 % CT, n % 2
                dve.wait_ge(piece_in[n % BUFS], 16 * (n // BUFS + 1))
                for i in range(PER):
                    at = (half * PER + i) * 6
                    nc.vector.bn_stats(stats[:, ct, b, at:at + 6], pieces[:, n % BUFS, i * STAT:(i + 1) * STAT])\
                      .then_inc(stat_done, 1)
            dve.wait_ge(stat_done, LOADS * PER)
            for ct in range(CT):
                for b in range(BATCH):
                    last = nc.vector.bn_aggr(mean_sq[:, ct, b, :], stats[:, ct, b, :])
                    if (ct, b) != (CT - 1, BATCH - 1):
                        link(last)
            link(last)
            link(nc.vector.tensor_tensor(square[:, :, :], mean_sq[:, :, :, 0], mean_sq[:, :, :, 0], ALU.mult))
            nc.vector.tensor_tensor(mean_sq[:, :, :, 1], mean_sq[:, :, :, 1], square[:, :, :], ALU.add).then_inc(summed, 1)
            dve.wait_ge(grouped, 1)
            link(nc.vector.tensor_copy(group[:, :, :], g_ps[0:NG, 0:2 * BATCH].rearrange("p (b k) -> p b k", k=2)))
            link(nc.vector.tensor_tensor(gsq[:, :], group[:, :, 0], group[:, :, 0], ALU.mult))
            link(nc.vector.tensor_tensor(group[:, :, 1], group[:, :, 1], gsq[:, :], ALU.subtract))
            nc.vector.tensor_scalar(group[:, :, 1], group[:, :, 1], EPS, None, ALU.add).then_inc(summed, 1)
            dve.wait_ge(rooted, 1)
            link(nc.vector.reciprocal(gsq[:, :], gsq[:, :]))
            link(nc.vector.tensor_tensor(newton[:, :], gsq[:, :], gsq[:, :], ALU.mult))
            link(nc.vector.tensor_tensor(newton[:, :], newton[:, :], group[:, :, 1], ALU.mult))
            link(nc.vector.tensor_scalar(newton[:, :], newton[:, :], -0.5, 1.5, ALU.mult, ALU.add))
            nc.vector.tensor_tensor(group[:, :, 1], gsq[:, :], newton[:, :], ALU.mult).then_inc(summed, 1)
            dve.wait_ge(spread, 1)
            link(nc.vector.tensor_copy(mean_rstd[:, :, :, :],
                                       b_ps[:, 0:CT * BATCH * 2].rearrange("p (t b k) -> p t b k", b=BATCH, k=2)))

        @block.scalar
        def _(act):
            act.wait_ge(summed, 2)
            nc.scalar.activation(gsq[:, :], group[:, :, 1], ACT.Sqrt).then_inc(rooted, 1)

        @block.tensor
        def _(pe):
            pe.wait_ge(const_in, 32)
            pe.wait_ge(summed, 1)
            for ct in range(CT):
                last = nc.tensor.matmul(g_ps[0:NG, 0:2 * BATCH], to_g[:, ct, :],
                                        mean_sq[:, ct, :, :].rearrange("p b k -> p (b k)"), start=ct == 0, stop=ct == CT - 1)
            last.then_inc(grouped, 1)
            pe.wait_ge(summed, 3)
            for ct in range(CT):
                last = nc.tensor.matmul(b_ps[:, ct * 2 * BATCH:(ct + 1) * 2 * BATCH], from_g[:, ct * LANES:(ct + 1) * LANES],
                                        group[:, :, :].rearrange("p b k -> p (b k)"), start=True, stop=True)
            last.then_inc(spread, 1)


def project_and_window_attention(nc, x, w_hi_qkv, w_lo_q, w_lo_kv, ident_dram, mean_rstd,
                                 q_dram, k_dram, v_dram, win_dram):
    f32, f16 = mybir.dt.float32, mybir.dt.float16
    ALU, ACT, AX = mybir.AluOpType, mybir.ActivationFunctionType, mybir.AxisListType
    BATCH, C = x.shape[0], x.shape[1]
    LANES, D, H, WN, IMW = 128, 32, 6, 4, 96
    CT = C // LANES
    CHUNKS = q_dram.shape[1]
    N = BATCH * CHUNKS
    TOK = x.shape[2] // CHUNKS
    WIN = TOK // WN
    WT = WIN // LANES
    HD = H * D
    M = 3 * D
    WCOL = 6 * HD
    QKV, LQ, LKV = 0, 3 * HD, 4 * HD
    SCALE = float(D) ** -0.5
    W_UP = 64.0
    BANK = 512
    AHEAD = [(0, 1), (2,), ()]
    UNITS, RING = 28, 7

    with ExitStack() as ctx:
        def sb(name, shape, dt=f32):
            return ctx.enter_context(nc.sbuf_tensor(name, shape, dt))

        def sem(name):
            return ctx.enter_context(nc.semaphore(name))

        x_in_sb = sb("x_in_sb", [LANES, 2, CT, TOK])
        xn = sb("xn", [LANES, CT, TOK])
        xh, xl = sb("xh", [LANES, 2 * CT * TOK], f16), sb("xl", [LANES, 2 * CT * TOK], f16)
        pool4 = sb("pool4", [LANES, CT, WIN])
        pool_mean = sb("pool_mean", [LANES, CT, WIN])
        ph, pl = sb("ph", [LANES, CT, WIN], f16), sb("pl", [LANES, CT, WIN], f16)
        wh, wl = sb("wh", [LANES, CT, WCOL], f16), sb("wl", [LANES, CT, WCOL], f16)
        ident = sb("ident", [LANES, LANES])
        qkv = sb("qkv", [LANES, WT, WN, 3 * HD])
        prod_s = sb("prod_s", [LANES, WN * WN, HD])
        prod_v = sb("prod_v", [LANES, WN, WN, HD])
        scores = sb("scores", [LANES, WN, WN, H])
        win_max, win_sum = sb("win_max", [LANES, WN, H]), sb("win_sum", [LANES, WN, H])
        probs_e = sb("probs_e", [LANES, WN, WN, H])
        probs_w = sb("probs_w", [LANES, WN, WN, H])
        win_out = sb("win_out", [LANES, WN, HD])
        win_t = sb("win_t", [M, 2, BANK])
        q_st = sb("q_st", [M, 2, 2, TOK], f16)
        k_st = sb("k_st", [M, 2, 2, WIN], f16)
        v_st = sb("v_st", [LANES, WT, HD])
        w_stage = qkv[:, :, :, :].rearrange("p a b c -> p (a b c)")[:, 0:CT * WCOL].rearrange("p (t n) -> p t n", t=CT)
        ring_ps = ctx.enter_context(nc.psum_tensor("ring_ps", [LANES, RING, BANK], f32))
        t_ps = ctx.enter_context(nc.psum_tensor("t_ps", [LANES, BANK], f32))

        w_in, w_hi_set, w_set = sem("w_in"), sem("w_hi_set"), sem("w_set")
        x_loaded, xn_done, xh_done, xl_done = sem("x_loaded"), sem("xn_done"), sem("xh_done"), sem("xl_done")
        pool_step, pool_mean_done, ph_done, pl_done = sem("pool_step"), sem("pool_mean_done"), sem("ph_done"), sem("pl_done")
        unit_done, act_evac, dve_evac = sem("unit_done"), sem("act_evac"), sem("dve_evac")
        hi_step, sub_done, exp_done_w, probs_done = sem("hi_step"), sem("sub_done"), sem("exp_done_w"), sem("probs_done")
        prod_v_done, win_done, t_done, t_evac = sem("prod_v_done"), sem("win_done"), sem("t_done"), sem("t_evac")
        q_saved, kv_saved, win_saved = sem("q_saved"), sem("kv_saved"), sem("win_saved")
        block = ctx.enter_context(nc.Block())

        units = []
        for wt in range(WT):
            units += [("qk", wt, i) for i in range(WN)] + [("v", wt, i) for i in range(2)]
            if wt < 2:
                units += [("lq", wt, i) for i in range(3)]
            else:
                units += [("lk", wt, i) for i in range(2)] + [("lv", wt, i) for i in range(2)]
        assert len(units) == UNITS and UNITS % RING == 0
        DVE_UNITS = [n for n, u in enumerate(units) if u[0] in ("lq", "lk")]
        ND = len(DVE_UNITS)

        def half(buf, s):
            return buf[:, bass.ds(s % 2 * (CT * TOK), CT * TOK)].rearrange("p (t i w) -> p t i w", t=CT, i=WN)

        @block.sync
        def _(sp):
            def load_x(s):
                if not isinstance(s, int) or s > 0:
                    sp.wait_ge(x_loaded, 48 * s)
                src = x[bass.ds(s // CHUNKS, 1), :, bass.ds(s % CHUNKS * TOK, TOK)][0]
                for ct in range(CT):
                    dst = x_in_sb[:, :, :, :].rearrange("p a t n -> p (a t n)")[:, bass.ds(s % 2 * (CT * TOK) + ct * TOK, TOK)]
                    sp.dma_start(dst, src[ct * LANES:(ct + 1) * LANES, :]).then_inc(x_loaded, 16)

            def save_window(turn):
                sp.wait_ge(t_evac, 2 * (turn + 2))
                for kt in range(2):
                    sp.dma_start(win_dram[bass.ds(turn, 1)][0, kt], win_t[:, kt, :]).then_inc(win_saved, 16)

            def save_chunk(s):
                b, c = s // CHUNKS, s % CHUNKS
                for wt in range(WT):
                    save_window(WT * s + wt)
                    if wt < 2:
                        sp.wait_ge(dve_evac, ND * (s + 1) + 3 * (wt + 1))
                        for part in range(2):
                            dst = q_dram[bass.ds(b, 1), bass.ds(c, 1), part, wt * 3:wt * 3 + 3][0, 0].rearrange("h d n -> (h d) n")
                            sp.dma_start(dst, q_st[:, wt, part, :]).then_inc(q_saved, 16)
                    else:
                        sp.wait_ge(dve_evac, ND * (s + 1) + ND)
                        for mt in range(2):
                            for part in range(2):
                                dst = k_dram[bass.ds(b, 1), part, mt * 3:mt * 3 + 3, :, bass.ds(c * WIN, WIN)][0]
                                sp.dma_start(dst.rearrange("h d n -> (h d) n"), k_st[:, mt, part, :]).then_inc(kv_saved, 16)
                        sp.wait_ge(act_evac, UNITS * (s + 1) + RING)
                        for w in range(WT):
                            dst = v_dram[bass.ds(b, 1), :, :, bass.ds(c * WT * D + w * D, D)][0].rearrange("h p d -> p h d")
                            sp.dma_start(dst, v_st[:, w, :].rearrange("p (h d) -> p h d", d=D)).then_inc(kv_saved, 16)

            sp.dma_start(w_stage[:, :, QKV:QKV + 3 * HD], w_hi_qkv.rearrange("(t p) n -> p t n", p=LANES)).then_inc(w_in, 16)
            sp.dma_start(w_stage[:, :, LQ:LQ + HD], w_lo_q.rearrange("(t p) n -> p t n", p=LANES)).then_inc(w_in, 16)
            sp.dma_start(w_stage[:, :, LKV:LKV + 2 * HD], w_lo_kv.rearrange("(t p) n -> p t n", p=LANES)).then_inc(w_in, 16)
            sp.dma_start(ident[:, :], ident_dram).then_inc(w_in, 16)
            load_x(0)
            load_x(1)
            with sp.Fori(0, N - 2) as s:
                sp.wait_ge(xn_done, CT * (s + 1))
                load_x(s + 2)
                save_chunk(s)
            with sp.Fori(N - 2, N) as s:
                save_chunk(s)
            save_window(WT * N)
            save_window(WT * N + 1)
            sp.wait_ge(win_saved, 32 * (WT * N + 3))
            sp.wait_ge(q_saved, 64 * (N + 1))
            sp.wait_ge(kv_saved, 112 * (N + 1))

        @block.tensor
        def _(pe):
            def unit(s, n):
                kind, wt, i = units[n]
                pe.wait_ge(act_evac, UNITS * s + n + 1)
                old = (n - RING) % UNITS
                if old in DVE_UNITS:
                    pe.wait_ge(dve_evac, ND * (s + (n >= RING)) + DVE_UNITS.index(old) + 1)
                bank = n % RING
                h, l = half(xh, s), half(xl, s)
                hh, hl, lh = (0, 0), (0, 1), (1, 0)
                if kind in ("qk", "v"):
                    runs = [(i, 0, QKV, 2 * HD)] if kind == "qk" else [(2 * i, 0, QKV + 2 * HD, HD), (2 * i + 1, HD, QKV + 2 * HD, HD)]
                    for place, to, col, width in runs:
                        terms = [(ct, a, b) for ct in range(CT) for a, b in (hh, hl, lh)]
                        for m, (ct, a, b) in enumerate(terms):
                            last = nc.tensor.matmul(ring_ps[:, bank, to:to + width],
                                                    (h, l)[a][:, ct, place, wt * LANES:(wt + 1) * LANES],
                                                    (wh, wl)[b][:, ct, col:col + width], start=m == 0, stop=m == len(terms) - 1)
                elif kind == "lv":
                    for w in ((0, 1), (2,))[i]:
                        terms = [(ct, a, b) for ct in range(CT) for a, b in (hh, hl, lh)]
                        for m, (ct, a, b) in enumerate(terms):
                            last = nc.tensor.matmul(ring_ps[:, bank, w % 2 * HD:w % 2 * HD + HD],
                                                    (ph, pl)[a][:, ct, w * LANES:(w + 1) * LANES],
                                                    (wh, wl)[b][:, ct, LKV + HD:LKV + 2 * HD], start=m == 0, stop=m == len(terms) - 1)
                else:
                    terms = [(ct, a, b) for ct in range(CT) for a, b in (hh, hl, lh)]
                    for m, (ct, a, b) in enumerate(terms):
                        if kind == "lq":
                            col = LQ + wt * M
                            moving = (h, l)[b][:, ct].rearrange("p i w -> p (i w)")[:, i * BANK:(i + 1) * BANK]
                        else:
                            col = LKV + i * M
                            moving = (ph, pl)[b][:, ct, :]
                        width = BANK if kind == "lq" else WIN
                        last = nc.tensor.matmul(ring_ps[0:M, bank, 0:width], (wh, wl)[a][:, ct, col:col + M], moving,
                                                start=m == 0, stop=m == len(terms) - 1)
                last.then_inc(unit_done, 1)

            def transposes(turn):
                pe.wait_ge(win_done, turn + 1)
                for kt in range(2):
                    pe.wait_ge(t_evac, 2 * turn + kt + 2)
                    for i in range(WN):
                        last = nc.tensor.transpose(t_ps[0:M, i * LANES:(i + 1) * LANES], win_out[:, i, kt * M:(kt + 1) * M], ident[:, :])
                    last.then_inc(t_done, 1)

            pe.wait_ge(w_set, 1)
            pe.sem_inc(unit_done, UNITS)
            pe.sem_inc(t_done, 2)
            with pe.Fori(0, N) as s:
                pe.wait_ge(xh_done, CT * (s + 2))
                pe.wait_ge(xl_done, CT * (s + 2))
                for wt in range(WT):
                    mine = [n for n in range(UNITS) if units[n][1] == wt]
                    for n in mine[:6]:
                        unit(s, n)
                    transposes(WT * s + wt)
                    if wt == WT - 1:
                        pe.wait_ge(ph_done, s + 1)
                        pe.wait_ge(pl_done, s + 1)
                    for n in mine[6:]:
                        unit(s, n)
            transposes(WT * N)
            transposes(WT * N + 1)

        @block.scalar
        def _(act):
            def evac(s, n):
                kind, wt, i = units[n]
                act.wait_ge(unit_done, UNITS * (s + 1) + n + 1)
                src = ring_ps[:, n % RING, :]
                if kind == "qk":
                    if i == 0:
                        act.wait_ge(prod_v_done, WT * s + wt + 1)
                    ins = nc.scalar.mul(qkv[:, wt, i, 0:2 * HD], src[:, 0:2 * HD], 1 / W_UP)
                elif kind == "v":
                    ins = nc.scalar.mul(qkv[:, wt, 2 * i:2 * i + 2, 2 * HD:3 * HD], src[:, 0:2 * HD].rearrange("p (a n) -> p a n", a=2), 1 / W_UP)
                elif kind == "lq":
                    act.wait_ge(q_saved, 64 * (s + 1))
                    ins = nc.scalar.mul(q_st[:, wt, 0, i * BANK:(i + 1) * BANK], src[0:M, :], 1 / W_UP)
                elif kind == "lk":
                    act.wait_ge(kv_saved, 112 * (s + 1))
                    ins = nc.scalar.mul(k_st[:, i, 0, :], src[0:M, 0:WIN], 1 / W_UP)
                elif i == 0:
                    ins = nc.scalar.mul(v_st[:, 0:2, :], src[:, 0:2 * HD].rearrange("p (a n) -> p a n", a=2), 1 / W_UP)
                else:
                    ins = nc.scalar.mul(v_st[:, 2, :], src[:, 0:HD], 1 / W_UP)
                ins.then_inc(act_evac, 1)

            def high_part(u, ct):
                act.wait_ge(xn_done, CT * u + ct + 1)
                if not isinstance(u, int):
                    act.wait_ge(unit_done, UNITS * u)
                nc.scalar.copy(half(xh, u)[:, ct], xn[:, ct, :].rearrange("p (i w) -> p i w", i=WN)).then_inc(xh_done, 1)

            def t_out(turn):
                for kt in range(2):
                    act.wait_ge(t_done, 2 * (turn + 1) + kt + 1)
                    if kt == 0:
                        act.wait_ge(win_saved, 32 * (turn + 1))
                    nc.scalar.copy(win_t[:, kt, :], t_ps[0:M, :]).then_inc(t_evac, 1)

            def turn(s, wt, ahead):
                for n in range(UNITS):
                    if units[n][1] == wt and units[n][0] in ("qk", "v"):
                        evac(s, n)
                t_out(WT * s + wt)
                for n in range(UNITS):
                    if units[n][1] == wt and units[n][0] not in ("qk", "v"):
                        evac(s, n)
                act.wait_ge(sub_done, WT * s + wt + 1)
                nc.scalar.activation(probs_e[:, :, :, :], scores[:, :, :, :], ACT.Exp, scale=SCALE).then_inc(exp_done_w, 1)
                if wt == 1:
                    act.wait_ge(pool_mean_done, s + 1)
                    act.wait_ge(unit_done, UNITS * (s + 1))
                    nc.scalar.copy(ph[:, :, :], pool_mean[:, :, :]).then_inc(ph_done, 1)
                if ahead:
                    for ct in AHEAD[wt]:
                        high_part(s + 1, ct)

            act.wait_ge(w_in, 64)
            nc.scalar.mul(wh[:, :, :], w_stage, W_UP).then_inc(w_hi_set, 1)
            act.sem_inc(act_evac, RING)
            act.sem_inc(t_evac, 2)
            act.sem_inc(xh_done, CT)
            act.sem_inc(win_saved, 32)
            act.sem_inc(q_saved, 64)
            act.sem_inc(kv_saved, 112)
            for ct in range(CT):
                high_part(0, ct)
            with act.Fori(0, N - 1) as s:
                for wt in range(WT):
                    turn(s, wt, True)
            for wt in range(WT):
                turn(N - 1, wt, False)
            t_out(WT * N)
            t_out(WT * N + 1)

        @block.gpsimd
        def _(pool):
            def low_part(u, ct):
                base = 4 * (CT * u + ct)
                pool.wait_ge(xh_done, CT * (u + 1) + ct + 1)
                view = xn[:, ct, :].rearrange("p (i w) -> p i w", i=WN)
                nc.gpsimd.tensor_tensor(half(xl, u)[:, ct], view, half(xh, u)[:, ct], ALU.subtract).then_inc(pool_step, 1)
                for i in range(1, WN):
                    pool.wait_ge(pool_step, base + i)
                    first = view[:, 0] if i == 1 else pool4[:, ct, :]
                    nc.gpsimd.tensor_tensor(pool4[:, ct, :], first, view[:, i], ALU.add).then_inc(pool_step, 1)
                pool.wait_ge(pool_step, base + 4)
                pool.sem_inc(xl_done, 1)

            def pooled_mean(s):
                nc.gpsimd.tensor_scalar(pool_mean[:, :, :], pool4[:, :, :], 1 / WN, None, ALU.mult).then_inc(pool_mean_done, 1)
                pool.wait_ge(pool_mean_done, s + 1)

            def pooled_low(s):
                pool.wait_ge(ph_done, s + 1)
                nc.gpsimd.tensor_tensor(pl[:, :, :], pool_mean[:, :, :], ph[:, :, :], ALU.subtract).then_inc(pl_done, 1)

            def windows(s, wt):
                pool.wait_ge(probs_done, WT * s + wt + 1)
                for i in range(WN):
                    p = probs_w[:, i, :, :].unsqueeze(3).broadcast_to([LANES, WN, H, D])
                    v = qkv[:, wt, :, 2 * HD:3 * HD].rearrange("p j (h d) -> p j h d", d=D)
                    last = nc.gpsimd.tensor_tensor(prod_v[:, i, :, :].rearrange("p j (h d) -> p j h d", d=D), p, v, ALU.mult)
                last.then_inc(prod_v_done, 1)

            nc.gpsimd.memset(prod_v[:, :, :, :].rearrange("p a b c -> p (a b c)"), 0.0).then_inc(prod_v_done, 1)
            pool.sem_inc(prod_v_done, WT - 1)
            pool.sem_inc(xl_done, CT)
            for ct in range(CT):
                low_part(0, ct)
            with pool.Fori(0, N - 1) as s:
                for wt in range(WT):
                    windows(s, wt)
                    if wt == 0:
                        pooled_mean(s)
                    if wt == 1:
                        pooled_low(s)
                    for ct in AHEAD[wt]:
                        low_part(s + 1, ct)
            for wt in range(WT):
                windows(N - 1, wt)
                if wt == 0:
                    pooled_mean(N - 1)
                if wt == 1:
                    pooled_low(N - 1)

        @block.vector
        def _(dve):
            SMALL = 5
            def normalise(u, ct):
                dve.wait_ge(x_loaded, 48 * (u + 1))
                dve.wait_ge(xh_done, CT * u + ct + 1)
                dve.wait_ge(xl_done, CT * u + ct + 1)
                b = u // CHUNKS
                flat = x_in_sb[:, :, :, :].rearrange("p a t n -> p (a t n)")
                src = flat[:, bass.ds(u % 2 * (CT * TOK) + ct * TOK, TOK)].rearrange(
                    "p (wy dy wx dx) -> p dy dx wy wx", dy=2, dx=2, wx=IMW // 2)
                dst = xn[:, ct, :].rearrange("p (dy dx wy wx) -> p dy dx wy wx", dy=2, dx=2, wx=IMW // 2)
                scal = mean_rstd[:, :, :, :].rearrange("p t b k -> p (t b k)")
                mean, rstd = (scal[:, bass.ds(ct * 2 * BATCH + b * 2 + k, 1)] for k in range(2))
                for dy in range(2):
                    last = nc.vector.tensor_scalar(dst[:, dy], src[:, dy], mean, rstd, ALU.subtract, ALU.mult)
                last.then_inc(xn_done, 1)

            def low_evac(s, n):
                kind, wt, i = units[n]
                j = DVE_UNITS.index(n)
                dve.wait_ge(act_evac, UNITS * s + n + 1 + RING)
                if kind == "lq":
                    at = slice(i * BANK, (i + 1) * BANK)
                    ins = nc.vector.scalar_tensor_tensor(q_st[:, wt, 1, at], ring_ps[0:M, n % RING, :], 1 / W_UP, q_st[:, wt, 0, at],
                                                         ALU.mult, ALU.subtract)
                else:
                    ins = nc.vector.scalar_tensor_tensor(k_st[:, i, 1, :], ring_ps[0:M, n % RING, 0:WIN], 1 / W_UP, k_st[:, i, 0, :],
                                                         ALU.mult, ALU.subtract)
                ins.then_inc(dve_evac, 1)

            def finish(turn):
                dve.wait_ge(prod_v_done, turn + WT)
                dve.wait_ge(t_done, 2 * (turn + 2))
                nc.vector.tensor_reduce(win_out[:, :, :], prod_v[:, :, :, :].rearrange("p i j n -> p i n j"), AX.X, ALU.add).then_inc(win_done, 1)

            def windows(s, wt, ahead):
                turn = WT * s + wt
                n_hi = max(n for n in range(UNITS) if units[n][1] == wt and units[n][0] == "v")
                dve.wait_ge(act_evac, UNITS * s + n_hi + 1 + RING)
                q = qkv[:, wt, :, 0:HD].unsqueeze(2).broadcast_to([LANES, WN, WN, HD])
                k = qkv[:, wt, :, HD:2 * HD].unsqueeze(1).broadcast_to([LANES, WN, WN, HD])
                base = SMALL * turn
                nc.vector.tensor_tensor(prod_s[:, :, :].rearrange("p (i j) n -> p i j n", j=WN), q, k, ALU.mult).then_inc(hi_step, 1)
                dve.wait_ge(hi_step, base + 1)
                nc.vector.tensor_reduce(scores[:, :, :, :].rearrange("p i j h -> p (i j h)"),
                                        prod_s[:, :, :].rearrange("p a (h d) -> p (a h) d", d=D), AX.X, ALU.add).then_inc(hi_step, 1)
                dve.wait_ge(hi_step, base + 2)
                nc.vector.tensor_reduce(win_max[:, :, :], scores[:, :, :, :].rearrange("p i j h -> p i h j"), AX.X, ALU.max).then_inc(hi_step, 1)
                dve.wait_ge(hi_step, base + 3)
                nc.vector.tensor_tensor(scores[:, :, :, :], scores[:, :, :, :],
                                        win_max[:, :, :].unsqueeze(2).broadcast_to([LANES, WN, WN, H]), ALU.subtract).then_inc(sub_done, 1)
                for n in DVE_UNITS:
                    if units[n][1] == wt:
                        low_evac(s, n)
                finish(turn)
                dve.wait_ge(exp_done_w, turn + 1)
                nc.vector.tensor_reduce(win_sum[:, :, :], probs_e[:, :, :, :].rearrange("p i j h -> p i h j"), AX.X, ALU.add).then_inc(hi_step, 1)
                dve.wait_ge(hi_step, base + 4)
                nc.vector.reciprocal(win_sum[:, :, :], win_sum[:, :, :]).then_inc(hi_step, 1)
                dve.wait_ge(hi_step, base + 5)
                nc.vector.tensor_tensor(probs_w[:, :, :, :], probs_e[:, :, :, :],
                                        win_sum[:, :, :].unsqueeze(2).broadcast_to([LANES, WN, WN, H]), ALU.mult).then_inc(probs_done, 1)
                if ahead:
                    for ct in AHEAD[wt]:
                        normalise(s + 1, ct)

            dve.wait_ge(w_hi_set, 1)
            nc.vector.scalar_tensor_tensor(wl[:, :, :], w_stage, W_UP, wh[:, :, :], ALU.mult, ALU.subtract).then_inc(w_set, 1)
            nc.vector.memset(win_out[:, :, :], 0.0).then_inc(win_done, 1)
            dve.sem_inc(dve_evac, ND)
            for ct in range(CT):
                normalise(0, ct)
            with dve.Fori(0, N - 1) as s:
                for wt in range(WT):
                    windows(s, wt, True)
            for wt in range(WT):
                windows(N - 1, wt, False)
            finish(WT * N)


def global_attention(nc, q_dram, k_dram, v_dram, m_dram, o_dram):
    f32, f16 = mybir.dt.float32, mybir.dt.float16
    ALU, ACT, AX = mybir.AluOpType, mybir.ActivationFunctionType, mybir.AxisListType
    BATCH, CHUNKS, D, QT = q_dram.shape[0], q_dram.shape[1], 32, q_dram.shape[5]
    HEADS, KEYS = q_dram.shape[3], k_dram.shape[4]
    LANES = 128
    GROUPS = BATCH * HEADS
    TILES = GROUPS * CHUNKS
    KB = KEYS // LANES
    QB = QT // LANES
    QUARTER = QT // 4
    BANK = 512
    UNITS = KB * QT // BANK
    CHUNK_UNITS = [2] * (UNITS // 2 - 1) + [1, 1]
    NCH = len(CHUNK_UNITS)
    CHUNK_START = [sum(CHUNK_UNITS[:k]) for k in range(NCH)]
    RING = 6
    SCALE = float(D) ** -0.5
    STEP = 64.0
    POOL_KB = [0, 1, 2, 4, 5, 7, 8, 10, 11, 13, 14]
    ADDS = len(POOL_KB) - 1
    SUM_KB = [b for b in range(KB) if b not in POOL_KB]
    added = {b: max(n, 1) for n, b in enumerate(POOL_KB)}
    MAXU = QB * KEYS // BANK
    last_chunk = {b: max(k for k in range(NCH) if CHUNK_START[k] * BANK < (b + 1) * QT) for b in range(KB)}

    with ExitStack() as ctx:
        def sb(name, shape, dt):
            return ctx.enter_context(nc.sbuf_tensor(name, shape, dt))

        def sem(name):
            return ctx.enter_context(nc.semaphore(name))

        q_ring = sb("q_ring", [LANES, 4 * QT], f16)
        k_ring = sb("k_ring", [LANES, 2 * KEYS], f16)
        v_ring = sb("v_ring", [LANES, 2 * KB * D], f32)
        v_now = sb("v_now", [LANES, KB * D], f32)
        ones = sb("ones32", [LANES, D], f32)
        probs = sb("probs", [LANES, RING * QT], f32)
        prob_sum = sb("prob_sum", [LANES, QT], f32)
        part_max = sb("part_max", [LANES, QB, 5], f32)
        tile_max = sb("tile_max", [LANES, 32], f32)
        max_rows = sb("max_rows", [LANES, 32], f32)
        max_split = sb("max_split", [LANES, 2, 32], f16)
        recip = sb("recip", [LANES, QUARTER], f32)
        o_norm = sb("o_norm", [LANES, QUARTER], f32)
        score_ps = ctx.enter_context(nc.psum_tensor("score_ps", [LANES, 4, BANK], f32))
        max_ps = ctx.enter_context(nc.psum_tensor("max_ps", [LANES, 2, BANK], f32))
        out_ps = ctx.enter_context(nc.psum_tensor("out_ps", [LANES, BANK], f32))
        sum_ps = ctx.enter_context(nc.psum_tensor("sum_ps", [LANES, BANK], f32))

        q_in, kv_in, m_in, m_saved = sem("q_in"), sem("kv_in"), sem("m_in"), sem("m_saved")
        consts_set, v_set, qk_done, exp_done = sem("consts_set"), sem("v_set"), sem("qk_done"), sem("exp_done")
        pv_done, adds_done, fold_done = sem("pv_done"), sem("adds_done"), sem("fold_done")
        maxqk_done, max_read, m_ready, o_ready = sem("maxqk_done"), sem("max_read"), sem("m_ready"), sem("o_ready")
        o_saved, dve_step, acc_step = sem("o_saved"), sem("dve_step"), sem("acc_step")
        block = ctx.enter_context(nc.Block())

        @block.sync
        def _(sp):
            def load_q(t):
                if not isinstance(t, int) or t > 0:
                    sp.wait_ge(q_in, 48 * t)
                src = q_dram[bass.ds((t // CHUNKS) // HEADS, 1), bass.ds(t % CHUNKS, 1), :, bass.ds((t // CHUNKS) % HEADS, 1)]
                for part, row in ((0, 0), (0, D), (1, 2 * D)):
                    sp.dma_start(q_ring[row:row + D, bass.ds(t % 4 * QT, QT)], src[0, 0, part, 0]).then_inc(q_in, 16)

            def load_kv(g):
                if not isinstance(g, int) or g > 0:
                    sp.wait_ge(kv_in, 64 * g)
                b, h = g // HEADS, g % HEADS
                src = k_dram[bass.ds(b, 1), :, bass.ds(h, 1)]
                for part, row in ((0, 0), (1, D), (0, 2 * D)):
                    sp.dma_start(k_ring[row:row + D, bass.ds(g % 2 * KEYS, KEYS)], src[0, part, 0]).then_inc(kv_in, 16)
                sp.dma_start(v_ring[:, bass.ds(g % 2 * KB * D, KB * D)], v_dram[bass.ds(b, 1), bass.ds(h, 1)][0, 0]).then_inc(kv_in, 16)

            def save_o(t):
                sp.wait_ge(o_ready, t + 2)
                dst = o_dram[bass.ds((t // CHUNKS) // HEADS, 1), bass.ds(t % CHUNKS, 1), bass.ds((t // CHUNKS) % HEADS * D, D)][0, 0]
                for quarter in range(4):
                    sp.dma_start(dst[:, quarter * QUARTER:(quarter + 1) * QUARTER],
                                 o_norm[quarter * D:(quarter + 1) * D, :]).then_inc(o_saved, 16)

            sp.sem_inc(o_saved, 64)
            load_kv(0)
            for t in range(3):
                load_q(t)
            with sp.Fori(0, GROUPS - 1) as g:
                for c in range(CHUNKS):
                    if c == 3:
                        load_kv(g + 1)
                    load_q(g * CHUNKS + c + 3)
                    save_o(g * CHUNKS + c)
            for c in range(CHUNKS):
                t = (GROUPS - 1) * CHUNKS + c
                if c < 3:
                    load_q(t + 3)
                save_o(t)
            sp.wait_ge(o_saved, 64 * (TILES + 1))

        @block.tensor
        def _(pe):
            def max_unit(t, j):
                pair, r = j // 9, j % 9
                pe.wait_ge(max_read, MAXU * t + j + 1)
                keys = t // CHUNKS % 2 * KEYS
                if r < 8:
                    parts = [(2 * pair + r // 4, (r % 4) * BANK, 0, BANK)]
                else:
                    parts = [(2 * pair, 4 * BANK, 0, KEYS - 4 * BANK), (2 * pair + 1, 4 * BANK, 256, KEYS - 4 * BANK)]
                for qb, at, to, n in parts:
                    last = nc.tensor.matmul(max_ps[:, j % 2, to:to + n], q_ring[0:3 * D, bass.ds(t % 4 * QT + qb * LANES, LANES)],
                                            k_ring[0:3 * D, bass.ds(keys + at, n)], start=True, stop=True)
                last.then_inc(maxqk_done, 1)

            def qk_chunk(t, k):
                pe.wait_ge(exp_done, NCH * t + k + 1)
                for i in range(CHUNK_UNITS[k]):
                    u = CHUNK_START[k] + i
                    kb, at = u * BANK // QT, u * BANK % QT
                    last = nc.tensor.matmul(score_ps[:, k % 2 * 2 + i, :],
                                            k_ring[0:3 * D + 2, bass.ds(t // CHUNKS % 2 * KEYS + kb * LANES, LANES)],
                                            q_ring[0:3 * D + 2, bass.ds(t % 4 * QT + at, BANK)], start=True, stop=True)
                last.then_inc(qk_done, 1)

            def pv(t, kb):
                pe.wait_ge(exp_done, NCH * t + last_chunk[kb] + 3)
                if kb == 0:
                    pe.wait_ge(v_set, t + 1)
                    pe.wait_ge(o_ready, t + 1)
                at = kb % RING * QT
                for quarter in range(4):
                    last = nc.tensor.matmul(out_ps[quarter * D:(quarter + 1) * D, 0:QUARTER], v_now[:, kb * D:(kb + 1) * D],
                                            probs[:, at + quarter * QUARTER:at + (quarter + 1) * QUARTER],
                                            start=kb == 0, stop=kb == KB - 1)
                if kb not in SUM_KB:
                    last.then_inc(pv_done, 1)

            def block_sum(t, kb):
                at = kb % RING * QT
                for quarter in range(4):
                    last = nc.tensor.matmul(sum_ps[quarter * D:(quarter + 1) * D, 0:QUARTER], ones[:, :],
                                            probs[:, at + quarter * QUARTER:at + (quarter + 1) * QUARTER],
                                            start=kb == SUM_KB[0], stop=False)
                last.then_inc(pv_done, 1)

            def fold(t):
                pe.wait_ge(adds_done, ADDS * (t + 2))
                for quarter in range(4):
                    last = nc.tensor.matmul(sum_ps[quarter * D:(quarter + 1) * D, 0:QUARTER], ones[:, :],
                                            prob_sum[:, quarter * QUARTER:(quarter + 1) * QUARTER], start=False, stop=True)
                last.then_inc(fold_done, 1)

            def attend(t, ahead):
                pe.wait_ge(m_in, 16 * (t + 1))
                steps = []
                pv_at = 0
                for k in range(NCH):
                    steps.append((CHUNK_UNITS[k], lambda k=k: qk_chunk(t, k)))
                    while pv_at < KB and last_chunk[pv_at] <= k - 2:
                        steps.append((3, lambda b=pv_at: pv(t, b)))
                        if pv_at in SUM_KB:
                            steps.append((3, lambda b=pv_at: block_sum(t, b)))
                        pv_at += 1
                for b in range(pv_at, KB):
                    steps.append((3, lambda b=b: pv(t, b)))
                    if b in SUM_KB:
                        steps.append((3, lambda b=b: block_sum(t, b)))
                steps.append((3, lambda: fold(t)))
                whole, done, unit = sum(n for n, _ in steps), 0, 0
                for n, step in steps:
                    step()
                    done += n
                    while ahead and unit * whole < done * MAXU:
                        max_unit(t + 2, unit)
                        unit += 1

            pe.wait_ge(consts_set, 2)
            with pe.Fori(0, 2) as t:
                pe.wait_ge(kv_in, 64)
                pe.wait_ge(q_in, 48 * (t + 1))
                for j in range(MAXU):
                    max_unit(t, j)
            with pe.Fori(0, TILES - 2) as t:
                pe.wait_ge(q_in, 48 * (t + 3))
                pe.wait_ge(kv_in, 64 * ((t + 2) // CHUNKS + 1))
                attend(t, True)
            with pe.Fori(TILES - 2, TILES) as t:
                attend(t, False)

        @block.scalar
        def _(act):
            def save_max(t):
                act.wait_ge(m_ready, t + 1)
                dst = m_dram[bass.ds(t, 1)][0]
                for i in range(4):
                    act.dma_start(dst[:, :, i, :], max_split[32 * i:32 * i + QB, :, :]).then_inc(m_saved, 16)

            def load_max(t):
                act.wait_ge(m_saved, 64 * (t + 2))
                src = m_dram[bass.ds(t, 1)][0].rearrange("c s i r -> s c i r")
                act.dma_start(q_ring[3 * D:3 * D + 2, bass.ds(t % 4 * QT, QT)].rearrange("s (c i r) -> s c i r", i=4, r=32),
                              src).then_inc(m_in, 16)

            def exps(t, ahead):
                g = t // CHUNKS
                act.wait_ge(kv_in, 64 * (g + 1))
                act.wait_ge(pv_done, KB * t + RING)
                nc.scalar.copy(v_now[:, :], v_ring[:, bass.ds(g % 2 * KB * D, KB * D)]).then_inc(v_set, 1)
                for k in range(NCH):
                    lo, hi = CHUNK_START[k] * BANK, (CHUNK_START[k] + CHUNK_UNITS[k]) * BANK
                    for kb in range(KB):
                        if lo <= kb * QT < hi:
                            act.wait_ge(pv_done, KB * t + kb + 1)
                            old = (kb - RING) % KB
                            if old in added:
                                act.wait_ge(adds_done, ADDS * (t + (kb >= RING)) + added[old])
                    act.wait_ge(qk_done, NCH * t + k + 1)
                    at = lo % (RING * QT)
                    nc.scalar.activation(probs[:, at:at + hi - lo],
                                         score_ps[:, k % 2 * 2:k % 2 * 2 + CHUNK_UNITS[k], :].rearrange("p a b -> p (a b)"),
                                         ACT.Exp, scale=SCALE).then_inc(exp_done, 1)
                    if ahead and k == 3:
                        save_max(t + 1)
                    if ahead and k == 12:
                        load_max(t + 1)

            act.sem_inc(exp_done, 2)
            act.sem_inc(pv_done, RING)
            act.sem_inc(m_saved, 64)
            save_max(0)
            load_max(0)
            with act.Fori(0, TILES - 1) as t:
                exps(t, True)
            exps(TILES - 1, False)

        @block.gpsimd
        def _(pool):
            nc.gpsimd.memset(ones[:, :], 1.0).then_inc(consts_set, 1)
            pool.wait_ge(consts_set, 1)
            nc.gpsimd.memset(k_ring[3 * D:3 * D + 2, :], STEP).then_inc(consts_set, 1)
            pool.sem_inc(adds_done, ADDS)
            with pool.Fori(0, TILES) as t:
                for n in range(1, ADDS + 1):
                    kb = POOL_KB[n]
                    pool.wait_ge(exp_done, NCH * t + last_chunk[kb] + 3)
                    if n == 1:
                        pool.wait_ge(fold_done, t + 1)
                    else:
                        pool.wait_ge(adds_done, ADDS * (t + 1) + n - 1)
                    first = probs[:, POOL_KB[0] % RING * QT:POOL_KB[0] % RING * QT + QT] if n == 1 else prob_sum[:, :]
                    nc.gpsimd.tensor_tensor(prob_sum[:, :], first, probs[:, kb % RING * QT:kb % RING * QT + QT],
                                            ALU.add).then_inc(adds_done, 1)

        @block.vector
        def _(dve):
            def reduce_units(t):
                for j in range(MAXU):
                    pair, r = j // 9, j % 9
                    dve.wait_ge(maxqk_done, MAXU * t + j + 1)
                    if j == 0:
                        dve.wait_ge(dve_step, 3 * t + 3)
                    if r < 8:
                        nc.vector.tensor_reduce(part_max[:, 2 * pair + r // 4, r % 4:r % 4 + 1], max_ps[:, j % 2, :],
                                                AX.X, ALU.max).then_inc(max_read, 1)
                    else:
                        nc.vector.tensor_reduce(part_max[:, 2 * pair:2 * pair + 2, 4],
                                                max_ps[:, j % 2, :].rearrange("p (a b) -> p a b", a=2),
                                                AX.X, ALU.max).then_inc(max_read, 1)
                dve.wait_ge(max_read, MAXU * (t + 1) + 2)
                nc.vector.tensor_reduce(tile_max[:, 0:QB], part_max[:, :, :], AX.X, ALU.max).then_inc(dve_step, 1)
                dve.wait_ge(dve_step, 3 * t + 4)
                dve.wait_ge(m_saved, 64 * (t + 1))
                nc.vector.transpose(max_rows[:, :], tile_max[:, :]).then_inc(dve_step, 1)
                dve.wait_ge(dve_step, 3 * t + 5)
                nc.vector.tensor_scalar(max_split[:, 0, :], max_rows[:, :], -1.0 / STEP, None, ALU.mult).then_inc(dve_step, 1)
                dve.wait_ge(dve_step, 3 * t + 6)
                nc.vector.scalar_tensor_tensor(max_split[:, 1, :], max_rows[:, :], -1.0 / STEP, max_split[:, 0, :],
                                               ALU.mult, ALU.subtract).then_inc(m_ready, 1)

            def normalise(t):
                dve.wait_ge(fold_done, t + 2)
                dve.wait_ge(o_ready, t + 1)
                nc.vector.reciprocal(recip[:, :], sum_ps[:, 0:QUARTER]).then_inc(acc_step, 1)
                dve.wait_ge(acc_step, t + 1)
                dve.wait_ge(o_saved, 64 * (t + 1))
                nc.vector.tensor_tensor(o_norm[:, :], out_ps[:, 0:QUARTER], recip[:, :], ALU.mult).then_inc(o_ready, 1)

            nc.vector.memset(tile_max[:, :], 0.0).then_inc(dve_step, 1)
            dve.sem_inc(dve_step, 2)
            dve.sem_inc(max_read, 2)
            dve.sem_inc(o_ready, 1)
            dve.sem_inc(fold_done, 1)
            with dve.Fori(0, 2) as t:
                reduce_units(t)
            with dve.Fori(0, TILES - 2) as t:
                reduce_units(t + 2)
                normalise(t)
            with dve.Fori(TILES - 2, TILES) as t:
                normalise(t)


def output_projections(nc, x, win_dram, o_dram, w_hi, w_lo, b_hi, b_lo, x1_dram, x1_stats):
    f32, f16 = mybir.dt.float32, mybir.dt.float16
    ALU, ACT = mybir.AluOpType, mybir.ActivationFunctionType
    BATCH, CHUNKS, HD, TOK = o_dram.shape
    N = BATCH * CHUNKS
    M, LANES, IMW, WN, STAT = 96, 128, 96, 4, 512
    KT = HD // M
    CG = 2 * KT
    WIN = TOK // WN
    WT = WIN // LANES
    W_UP = 64.0
    YR = 4
    PS = 8
    UNITS = CG * WN
    PIECES = TOK // STAT
    LOADS = WT * KT + KT + CG

    with ExitStack() as ctx:
        def sb(name, shape, dt=f32):
            return ctx.enter_context(nc.sbuf_tensor(name, shape, dt))

        def sem(name):
            return ctx.enter_context(nc.semaphore(name))

        att = sb("att", [M, 2 * 2 * KT * TOK])
        ah, al = sb("ah", [M, 2 * 2 * KT * TOK], f16), sb("al", [M, 2 * 2 * KT * TOK], f16)
        y = sb("y", [M, YR, WIN])
        xb = sb("xb", [M, 2 * CG * TOK])
        w_stage = sb("pw_stage", [M, 2, KT, HD])
        wh, wl = sb("pwh", [M, 2, KT, HD], f16), sb("pwl", [M, 2, KT, HD], f16)
        bias = sb("bias", [M, CG])
        stats = sb("x1_bn", [M, CG, N * PIECES * 6])
        ps = ctx.enter_context(nc.psum_tensor("proj_ps", [LANES, PS, 512], f32))
        w_in, w_hi_set, w_set = sem("pw_in"), sem("pw_hi_set"), sem("pw_set")
        in_done, high_done, low_done = sem("in_done"), sem("high_done"), sem("low_done")
        unit_done, added, evac, x1_saved, stat_done = sem("p_unit_done"), sem("added"), sem("p_evac"), sem("x1_saved"), sem("x1_stat_done")
        block = ctx.enter_context(nc.Block())

        def slot(buf, s, width, at, n):
            return buf[:, bass.ds(s % 2 * width + at, n)]

        @block.sync
        def _(sp):
            def load(s):
                b, c = s // CHUNKS, s % CHUNKS
                for kt in range(KT):
                    for wt in range(WT):
                        dst = slot(att, s, 2 * KT * TOK, kt * TOK, TOK).rearrange("p (i w) -> p i w", i=WN)
                        sp.dma_start(dst[:, :, wt * LANES:(wt + 1) * LANES],
                                     win_dram[bass.ds(s * WT + wt + 2, 1)][0, kt].rearrange("p (i w) -> p i w", i=WN)).then_inc(in_done, 16)
                    sp.dma_start(slot(att, s, 2 * KT * TOK, (KT + kt) * TOK, TOK),
                                 o_dram[bass.ds(b, 1), bass.ds(c, 1), kt * M:(kt + 1) * M][0, 0]).then_inc(in_done, 16)
                for g in range(CG):
                    sp.dma_start(slot(xb, s, CG * TOK, g * TOK, TOK),
                                 x[bass.ds(b, 1), g * M:(g + 1) * M, bass.ds(c * TOK, TOK)][0]).then_inc(in_done, 16)

            for src, (w, bb) in enumerate(((w_hi, b_hi), (w_lo, b_lo))):
                sp.dma_start(w_stage[:, src, :, :], w.rearrange("(t p) n -> p t n", p=M)).then_inc(w_in, 16)
                for kt in range(KT):
                    sp.dma_start(bias[:, src * KT + kt:src * KT + kt + 1], bb[kt * M:(kt + 1) * M, :]).then_inc(w_in, 16)
            def save(s):
                for g in range(CG):
                    sp.wait_ge(stat_done, PIECES * (CG * s + g + 1))
                    sp.dma_start(x1_dram[bass.ds(s // CHUNKS, 1), g * M:(g + 1) * M, bass.ds(s % CHUNKS * TOK, TOK)][0],
                                 slot(xb, s, CG * TOK, g * TOK, TOK)).then_inc(x1_saved, 16)

            sp.sem_inc(x1_saved, 16 * CG)
            load(0)
            with sp.Fori(0, N - 1) as s:
                sp.wait_ge(x1_saved, 16 * CG * (s + 1))
                sp.wait_ge(in_done, 16 * LOADS * s + 16 * LOADS)
                load(s + 1)
                save(s)
            save(N - 1)
            sp.wait_ge(x1_saved, 16 * CG * (N + 1))

        @block.scalar
        def _(act):
            def high(s, src):
                act.wait_ge(in_done, 16 * LOADS * (s + 1))
                act.wait_ge(unit_done, UNITS * (s + 1))
                nc.scalar.copy(slot(ah, s, 2 * KT * TOK, src * KT * TOK, KT * TOK),
                               slot(att, s, 2 * KT * TOK, src * KT * TOK, KT * TOK)).then_inc(high_done, 1)

            def evacs(s):
                for u in range(UNITS):
                    act.wait_ge(unit_done, UNITS * (s + 2) + u + 1)
                    act.wait_ge(added, UNITS * s + u + 1)
                    nc.scalar.activation(y[:, u % YR, :], ps[0:M, u % PS, 0:WIN], ACT.Identity, bias=bias[:, u // WN:u // WN + 1],
                                         scale=1 / W_UP).then_inc(evac, 1)

            act.wait_ge(w_in, 16 * (2 + CG))
            nc.scalar.mul(wh[:, :, :, :], w_stage[:, :, :, :], W_UP).then_inc(w_hi_set, 1)
            act.sem_inc(evac, PS)
            high(0, 0)
            high(0, 1)
            with act.Fori(0, N - 1) as s:
                high(s + 1, 0)
                high(s + 1, 1)
                evacs(s)
            evacs(N - 1)

        @block.gpsimd
        def _(pool):
            with pool.Fori(0, N) as s:
                for src in range(2):
                    pool.wait_ge(high_done, 2 * s + src + 1)
                    at, n = src * KT * TOK, KT * TOK
                    nc.gpsimd.tensor_tensor(slot(al, s, 2 * KT * TOK, at, n), slot(att, s, 2 * KT * TOK, at, n),
                                            slot(ah, s, 2 * KT * TOK, at, n), ALU.subtract).then_inc(low_done, 1)

        @block.tensor
        def _(pe):
            pe.wait_ge(w_set, 1)
            pe.sem_inc(unit_done, 2 * UNITS)
            with pe.Fori(0, N) as s:
                for u in range(UNITS):
                    g, i = u // WN, u % WN
                    src, mt = g // KT, g % KT
                    if u % (UNITS // 2) == 0:
                        pe.wait_ge(high_done, 2 * s + src + 1)
                        pe.wait_ge(low_done, 2 * s + src + 1)
                    pe.wait_ge(evac, UNITS * s + u + 1)
                    terms = [(kt, a, b) for kt in range(KT) for a, b in ((0, 0), (0, 1), (1, 0))]
                    for m, (kt, a, b) in enumerate(terms):
                        last = nc.tensor.matmul(ps[0:M, u % PS, 0:WIN], (wh, wl)[a][:, src, kt, mt * M:(mt + 1) * M],
                                                slot((ah, al)[b], s, 2 * KT * TOK, (src * KT + kt) * TOK + i * WIN, WIN),
                                                start=m == 0, stop=m == len(terms) - 1)
                    last.then_inc(unit_done, 1)

        @block.vector
        def _(dve):
            dve.wait_ge(w_hi_set, 1)
            nc.vector.scalar_tensor_tensor(wl[:, :, :, :].rearrange("p a b c -> p (a b c)"), w_stage[:, :, :, :].rearrange("p a b c -> p (a b c)"),
                                           W_UP, wh[:, :, :, :].rearrange("p a b c -> p (a b c)"), ALU.mult, ALU.subtract).then_inc(w_set, 1)
            dve.sem_inc(added, YR)
            with dve.Fori(0, N) as s:
                for u in range(UNITS):
                    g, i = u // WN, u % WN
                    dve.wait_ge(evac, UNITS * s + u + 1 + PS)
                    view = slot(xb, s, CG * TOK, g * TOK, TOK).rearrange("p (wy dy wx dx) -> p dy dx wy wx", dy=2, dx=2, wx=IMW // 2)[:, i // 2, i % 2]
                    nc.vector.tensor_tensor(view, y[:, u % YR, :].rearrange("p (wy wx) -> p wy wx", wx=IMW // 2), view, ALU.add).then_inc(added, 1)
                    if i == WN - 1:
                        dve.wait_ge(added, UNITS * s + u + 1 + YR)
                        for k in range(PIECES):
                            out = stats[:, g, :][:, bass.ds((s * PIECES + k) * 6, 6)]
                            nc.vector.bn_stats(out, slot(xb, s, CG * TOK, g * TOK + k * STAT, STAT)).then_inc(stat_done, 1)
            dve.wait_ge(stat_done, N * CG * PIECES)
            for g in range(CG):
                for b in range(BATCH):
                    half = CHUNKS * PIECES * 6
                    nc.vector.bn_aggr(x1_stats[:, g, b, :], stats[:, g, b * half:(b + 1) * half])


def convolution_tables(nc, offset, difference, to_groups, eye, x1_stats, conv_norm, taps):
    f32 = mybir.dt.float32
    ALU, ACT, AX = mybir.AluOpType, mybir.ActivationFunctionType, mybir.AxisListType
    M, CG, BATCH = x1_stats.shape[0], x1_stats.shape[1], x1_stats.shape[2]
    NG = to_groups.shape[2]
    P = offset.shape[0]
    SIZE, REACH, SIGMA, EPS = M, 2, 0.5, 1e-5
    SHARP = -1.0 / (2.0 * SIGMA ** 2)
    MAGIC = 1.5 * 2.0 ** 23

    with ExitStack() as ctx:
        def sb(name, shape):
            return ctx.enter_context(nc.sbuf_tensor(name, shape, f32))

        def sem(name):
            return ctx.enter_context(nc.semaphore(name))

        off = sb("off", [M, P, 2])
        diff = sb("diff", [M, SIZE])
        to_g = sb("to_g96", [M, CG, NG])
        eye_sb = sb("eye_sb", [NG, NG])
        ones = sb("ones_g", [NG, M])
        mean_sq = sb("mean_sq1", [M, CG, BATCH, 2])
        square = sb("square1", [M, CG, BATCH])
        group = sb("group1", [NG, BATCH, 2])
        root, newton = sb("root1", [NG, BATCH]), sb("newton1", [NG, BATCH])
        diag = sb("diag", [NG, BATCH, 2, NG])
        whole, rest = sb("whole", [M, 2, P]), sb("rest", [M, 2, P])
        place, inside, norm = sb("place", [M, 2, P]), sb("inside", [M, 2, P]), sb("norm", [M, 2, P])
        five = sb("five", [M, 2, P, 2 * REACH + 1])
        dist = sb("dist", [M, P, SIZE])
        near = sb("near", [M, P, SIZE])
        g_ps = ctx.enter_context(nc.psum_tensor("g1_ps", [128, 512], f32))
        c_ps = ctx.enter_context(nc.psum_tensor("c1_ps", [128, 512], f32))
        c_in, step, to_act, from_act, to_pe, from_pe = (sem("t_in"), sem("t_step"), sem("t_to_act"), sem("t_from_act"),
                                                        sem("t_to_pe"), sem("t_from_pe"))
        block = ctx.enter_context(nc.Block())

        @block.sync
        def _(sp):
            sp.dma_start(off[:, :, :], offset.unsqueeze(0).broadcast_to([M, P, 2])).then_inc(c_in, 16)
            sp.dma_start(diff[:, :], difference).then_inc(c_in, 16)
            sp.dma_start(to_g[:, :, :], to_groups).then_inc(c_in, 16)
            sp.dma_start(eye_sb[:, :], eye).then_inc(c_in, 16)

        @block.tensor
        def _(pe):
            pe.wait_ge(to_pe, 1)
            for g in range(CG):
                last = nc.tensor.matmul(g_ps[0:NG, 0:2 * BATCH], to_g[:, g, :], mean_sq[:, g, :, :].rearrange("p b k -> p (b k)"),
                                        start=g == 0, stop=g == CG - 1)
            last.then_inc(from_pe, 1)
            pe.wait_ge(to_pe, 2)
            nc.tensor.matmul(c_ps[0:M, 0:2 * BATCH * NG], ones[:, :], diag[:, :, :, :].rearrange("g b k h -> g (b k h)"),
                             start=True, stop=True).then_inc(from_pe, 1)

        @block.scalar
        def _(act):
            act.wait_ge(to_act, 1)
            nc.scalar.activation(root[:, :], group[:, :, 1], ACT.Sqrt).then_inc(from_act, 1)
            act.wait_ge(to_act, 2)
            nc.scalar.activation(five[:, :, :, :], five[:, :, :, :], ACT.Exp, scale=SHARP).then_inc(from_act, 1)
            for axis in range(2):
                act.wait_ge(to_act, 3 + axis)
                nc.scalar.activation(dist[:, :, :], dist[:, :, :], ACT.Exp, scale=SHARP).then_inc(from_act, 1)

        @block.vector
        def _(dve):
            v = nc.vector
            count = [0]

            def link(ins):
                count[0] += 1
                ins.then_inc(step, 1)
                dve.wait_ge(step, count[0])

            def wide(ap):
                return ap.unsqueeze(2).broadcast_to([M, P, SIZE])

            dve.wait_ge(c_in, 64)
            link(v.memset(ones[:, :], 1.0))
            link(v.tensor_tensor(square[:, :, :], x1_stats[:, :, :, 0], x1_stats[:, :, :, 0], ALU.mult))
            link(v.tensor_copy(mean_sq[:, :, :, 0], x1_stats[:, :, :, 0]))
            v.tensor_tensor(mean_sq[:, :, :, 1], x1_stats[:, :, :, 1], square[:, :, :], ALU.add).then_inc(to_pe, 1)
            dve.wait_ge(from_pe, 1)
            link(v.tensor_copy(group[:, :, :], g_ps[0:NG, 0:2 * BATCH].rearrange("p (b k) -> p b k", k=2)))
            link(v.tensor_tensor(newton[:, :], group[:, :, 0], group[:, :, 0], ALU.mult))
            link(v.tensor_tensor(group[:, :, 1], group[:, :, 1], newton[:, :], ALU.subtract))
            v.tensor_scalar(group[:, :, 1], group[:, :, 1], EPS, None, ALU.add).then_inc(to_act, 1)
            dve.wait_ge(from_act, 1)
            link(v.reciprocal(root[:, :], root[:, :]))
            link(v.tensor_tensor(newton[:, :], root[:, :], root[:, :], ALU.mult))
            link(v.tensor_tensor(newton[:, :], newton[:, :], group[:, :, 1], ALU.mult))
            link(v.tensor_scalar(newton[:, :], newton[:, :], -0.5, 1.5, ALU.mult, ALU.add))
            link(v.tensor_tensor(group[:, :, 1], root[:, :], newton[:, :], ALU.mult))
            for b in range(BATCH):
                for k in range(2):
                    last = v.tensor_scalar(diag[:, b, k, :], eye_sb[:, :], group[:, b, k:k + 1], None, ALU.mult)
                    if (b, k) != (BATCH - 1, 1):
                        link(last)
            last.then_inc(to_pe, 1)
            dve.wait_ge(from_pe, 2)
            link(v.tensor_copy(conv_norm[:, :], c_ps[0:M, 0:2 * BATCH * NG]))
            o = off[:, :, :].rearrange("m p a -> m a p")
            link(v.tensor_scalar(whole[:, :, :], o, MAGIC, None, ALU.add))
            link(v.tensor_scalar(whole[:, :, :], whole[:, :, :], MAGIC, None, ALU.subtract))
            link(v.tensor_tensor(rest[:, :, :], o, whole[:, :, :], ALU.subtract))
            for u in range(2 * REACH + 1):
                link(v.tensor_scalar(five[:, :, :, u], rest[:, :, :], float(u - REACH), None, ALU.add))
            link(v.tensor_tensor(five[:, :, :, :], five[:, :, :, :], five[:, :, :, :], ALU.mult))
            dve.sem_inc(to_act, 1)
            dve.wait_ge(from_act, 2)
            link(v.tensor_reduce(norm[:, :, :], five[:, :, :, :], AX.X, ALU.add))
            link(v.reciprocal(norm[:, :, :], norm[:, :, :]))
            link(v.tensor_scalar(place[:, :, :], whole[:, :, :], diff[:, 0:1], None, ALU.add))
            link(v.tensor_scalar(inside[:, :, :], place[:, :, :], 0.0, None, ALU.is_ge))
            link(v.tensor_tensor(norm[:, :, :], norm[:, :, :], inside[:, :, :], ALU.mult))
            link(v.tensor_scalar(inside[:, :, :], place[:, :, :], float(SIZE - 1), None, ALU.is_le))
            link(v.tensor_tensor(norm[:, :, :], norm[:, :, :], inside[:, :, :], ALU.mult))
            for axis in range(2):
                link(v.tensor_tensor(dist[:, :, :], diff[:, :].unsqueeze(1).broadcast_to([M, P, SIZE]), wide(whole[:, axis, :]), ALU.add))
                link(v.tensor_scalar(near[:, :, :], dist[:, :, :], REACH + 0.5, None, ALU.is_le))
                link(v.scalar_tensor_tensor(near[:, :, :].rearrange("m p t -> m (p t)"), dist[:, :, :].rearrange("m p t -> m (p t)"),
                                            -(REACH + 0.5), near[:, :, :].rearrange("m p t -> m (p t)"), ALU.is_ge, ALU.mult))
                link(v.tensor_tensor(near[:, :, :], near[:, :, :], wide(norm[:, axis, :]), ALU.mult))
                link(v.tensor_tensor(dist[:, :, :], dist[:, :, :], wide(rest[:, axis, :]), ALU.add))
                link(v.tensor_tensor(dist[:, :, :], dist[:, :, :], dist[:, :, :], ALU.mult))
                dve.sem_inc(to_act, 1)
                dve.wait_ge(from_act, 3 + axis)
                link(v.tensor_tensor(taps[:, axis, :, :], dist[:, :, :], near[:, :, :], ALU.mult))


def displaced_convolution(nc, x1_dram, conv_norm, taps, out):
    f32 = mybir.dt.float32
    ALU = mybir.AluOpType
    BATCH, C = x1_dram.shape[0], x1_dram.shape[1]
    S, P = taps.shape[0], taps.shape[2]
    NG = conv_norm.shape[1] // (2 * BATCH)
    CP, CGRP = C // P, C // NG
    CH = 24
    POS, GRP = CH // CP, CH // CGRP
    PER = C // CH
    N = BATCH * PER
    SLOTS = 4
    W = CH * S
    BC = CP // 2

    with ExitStack() as ctx:
        def sb(name, shape):
            return ctx.enter_context(nc.sbuf_tensor(name, shape, f32))

        def sem(name):
            return ctx.enter_context(nc.semaphore(name))

        xc = sb("xc", [S, SLOTS, CH, S])
        xn = sb("xcn", [S, 2, CH, S])
        mid = sb("mid", [S, 2, CP, S])
        res = sb("res", [S, SLOTS, CH, S])
        mid_ps = ctx.enter_context(nc.psum_tensor("mid_ps", [128, 2, 2, 512], f32))
        out_ps = ctx.enter_context(nc.psum_tensor("conv_ps", [128, 2, 2, 512], f32))
        c_in, c_norm, first_done, mid_done = sem("c_in"), sem("c_norm"), sem("first_done"), sem("mid_done")
        second_done, res_done, c_out = sem("second_done"), sem("res_done"), sem("c_out")
        block = ctx.enter_context(nc.Block())

        def image(t, n):
            return t[bass.ds(n // PER, 1), bass.ds(n % PER * CH, CH)][0].rearrange("c (y x) -> y c x", y=S)

        @block.sync
        def _(sp):
            def load(n, slot):
                if not isinstance(n, int) or n > 0:
                    sp.wait_ge(c_in, 16 * n)
                sp.dma_start(xc[:, slot, :, :], image(x1_dram, n)).then_inc(c_in, 16)

            def store(n, slot):
                sp.wait_ge(res_done, POS * (n + 1) + 2)
                sp.dma_start(image(out, n), res[:, slot, :, :]).then_inc(c_out, 16)

            sp.sem_inc(c_out, 16 * SLOTS)
            for n in range(SLOTS - 1):
                load(n, n)
            with sp.Fori(0, N // SLOTS - 1) as turn:
                n = turn * SLOTS
                for k in range(SLOTS):
                    load(n + k + SLOTS - 1, (k + SLOTS - 1) % SLOTS)
                    store(n + k, k)
            for k in range(SLOTS):
                if k == 0:
                    load(N - 1, SLOTS - 1)
                store(N - SLOTS + k, k)
            sp.wait_ge(c_out, 16 * (N + SLOTS))

        @block.tensor
        def _(pe):
            def first(n, k, j):
                m = POS * k + j
                if j == 0:
                    pe.wait_ge(c_norm, GRP * (n + k + 1))
                pe.wait_ge(mid_done, POS * n + m + 1)
                table = taps[:, :, :, :].rearrange("s a p t -> s (a p t)")[:, bass.ds((P + (n + k) % PER * POS + j) * S, S)]
                for c in range(CP):
                    at = c % BC * S
                    last = nc.tensor.matmul(mid_ps[0:S, m % 2, c // BC, at:at + S], xn[:, k % 2, j * CP + c, :], table, start=True, stop=True)
                last.then_inc(first_done, 1)

            def second(n, k, j):
                m = POS * k + j
                pe.wait_ge(mid_done, POS * n + m + 3)
                pe.wait_ge(res_done, POS * n + m + 1)
                table = taps[:, :, :, :].rearrange("s a p t -> s (a p t)")[:, bass.ds(((n + k) % PER * POS + j) * S, S)]
                for c in range(CP):
                    at = c % BC * S
                    last = nc.tensor.matmul(out_ps[0:S, m % 2, c // BC, at:at + S], mid[:, m % 2, c, :], table, start=True, stop=True)
                last.then_inc(second_done, 1)

            pe.sem_inc(first_done, POS)
            with pe.Fori(0, N // SLOTS) as turn:
                n = turn * SLOTS
                order = [(k, j) for k in range(SLOTS) for j in range(POS)]
                first(n, *order[0])
                for i, (k, j) in enumerate(order):
                    if i + 1 < len(order):
                        first(n, *order[i + 1])
                    second(n, k, j)

        @block.scalar
        def _(act):
            act.sem_inc(mid_done, 2)
            act.sem_inc(second_done, 2)
            with act.Fori(0, N // SLOTS) as turn:
                n = turn * SLOTS
                for m in range(SLOTS * POS):
                    act.wait_ge(first_done, POS * (n + 1) + m + 1)
                    act.wait_ge(second_done, POS * n + m + 1)
                    nc.scalar.copy(mid[:, m % 2, :, :].rearrange("s (h c) t -> s h (c t)", h=2),
                                   mid_ps[0:S, m % 2, :, 0:BC * S]).then_inc(mid_done, 1)

        @block.vector
        def _(dve):
            def normalise(n, k):
                at = n + k
                dve.wait_ge(c_in, 16 * (at + 1))
                if not isinstance(at, int) or at > 0:
                    dve.wait_ge(first_done, POS * at)
                for g in range(GRP):
                    scale = [conv_norm[:, bass.ds((at // PER * 2 + kk) * NG + at % PER * GRP + g, 1)] for kk in range(2)]
                    nc.vector.tensor_scalar(xn[:, k % 2, g * CGRP:(g + 1) * CGRP, :], xc[:, k % SLOTS, g * CGRP:(g + 1) * CGRP, :],
                                            scale[0], scale[1], ALU.subtract, ALU.mult).then_inc(c_norm, 1)

            def finish(n, k):
                for j in range(POS):
                    m = POS * k + j
                    dve.wait_ge(second_done, POS * n + m + 3)
                    if j == 0:
                        dve.wait_ge(c_out, 16 * (n + k + 1))
                    span = slice(j * CP, (j + 1) * CP)
                    nc.vector.tensor_tensor(res[:, k, span, :].rearrange("s (h c) t -> s h (c t)", h=2), out_ps[0:S, m % 2, :, 0:BC * S],
                                            xc[:, k, span, :].rearrange("s (h c) t -> s h (c t)", h=2), ALU.add).then_inc(res_done, 1)

            dve.sem_inc(res_done, 2)
            normalise(0, 0)
            with dve.Fori(0, N // SLOTS - 1) as turn:
                n = turn * SLOTS
                for k in range(SLOTS):
                    normalise(n, k + 1)
                    finish(n, k)
            for k in range(SLOTS):
                if k + 1 < SLOTS:
                    normalise(N - SLOTS, k + 1)
                finish(N - SLOTS, k)


def displaced_attention_kernel(nc, x, w_hi_qkv, w_hi_proj, b_hi_proj, w_lo_q, w_lo_kv, w_lo_proj, b_lo_proj, offset,
                               to_groups, from_groups, to_groups96, identity, difference, out):
    f32, f16 = mybir.dt.float32, mybir.dt.float16
    BATCH, C, PIX = x.shape
    H, D, CHUNKS, SIZE = 6, 32, 6, 96
    TOK, KEYS = PIX // CHUNKS, PIX // 4
    NG, P = to_groups.shape[2], offset.shape[0]
    WTILES = BATCH * KEYS // 128

    def scratch(name, shape, dt):
        return nc.dram_tensor(name, shape, dt, kind="Internal").ap()

    q_dram = scratch("q_parts", [BATCH, CHUNKS, 2, H, D, TOK], f16)
    k_dram = scratch("k_parts", [BATCH, 2, H, D, KEYS], f16)
    v_dram = scratch("v_rows", [BATCH, H, 128, KEYS // 128 * D], f32)
    m_dram = scratch("maxima", [BATCH * H * CHUNKS, TOK // 128, 2, 4, 32], f16)
    o_dram = scratch("global_out", [BATCH, CHUNKS, H * D, TOK], f32)
    win_dram = scratch("window_out", [WTILES + 2, 2, 96, 512], f32)
    x1_dram = scratch("x1", [BATCH, C, PIX], f32)

    with ExitStack() as ctx:
        mean_rstd = ctx.enter_context(nc.sbuf_tensor("mean_rstd", [128, C // 128, BATCH, 2], f32))
        x1_stats = ctx.enter_context(nc.sbuf_tensor("x1_stats", [96, C // 96, BATCH, 2], f32))
        conv_norm = ctx.enter_context(nc.sbuf_tensor("conv_norm", [96, 2 * BATCH * NG], f32))
        group_scales(nc, x, to_groups, from_groups, mean_rstd)
        project_and_window_attention(nc, x, w_hi_qkv, w_lo_q, w_lo_kv, identity, mean_rstd, q_dram, k_dram, v_dram, win_dram)
        global_attention(nc, q_dram, k_dram, v_dram, m_dram, o_dram)
        output_projections(nc, x, win_dram, o_dram, w_hi_proj, w_lo_proj, b_hi_proj, b_lo_proj, x1_dram, x1_stats)
        taps = ctx.enter_context(nc.sbuf_tensor("taps", [SIZE, 2, P, SIZE], f32))
        convolution_tables(nc, offset, difference, to_groups96, identity[0:NG, 0:NG], x1_stats, conv_norm, taps)
        displaced_convolution(nc, x1_dram, conv_norm, taps, out)


def kernel(x, L0_conv_Wh_qkv, L0_conv_Wh_proj, L0_conv_bh_proj, L0_conv_Wl_q, L0_conv_Wl_kv, L0_conv_Wl_proj,
           L0_conv_bl_proj, L1_conv_offset):
    import numpy as np
    import concourse.bacc as bacc
    from concourse.bass_utils import run_bass_kernel_spmd

    x = np.ascontiguousarray(x)
    B, C, HH, WW = x.shape
    G = 32
    channel = np.arange(C)
    member = (channel[:, None] // (C // G) == np.arange(G)[None, :]).astype(np.float32)
    arrays = {
        "x": x.reshape(B, C, HH * WW),
        "w_hi_qkv": L0_conv_Wh_qkv, "w_hi_proj": L0_conv_Wh_proj, "b_hi_proj": L0_conv_bh_proj.reshape(-1, 1),
        "w_lo_q": L0_conv_Wl_q, "w_lo_kv": L0_conv_Wl_kv, "w_lo_proj": L0_conv_Wl_proj, "b_lo_proj": L0_conv_bl_proj.reshape(-1, 1),
        "offset": L1_conv_offset,
        "to_groups": (member * np.float32(G / C)).reshape(C // 128, 128, G).transpose(1, 0, 2),
        "from_groups": member.T,
        "to_groups96": (member * np.float32(G / C)).reshape(C // 96, 96, G).transpose(1, 0, 2),
        "identity": np.eye(128, dtype=np.float32),
        "difference": (np.arange(HH)[:, None] - np.arange(HH)[None, :]).astype(np.float32),
    }
    arrays = {name: np.ascontiguousarray(a) for name, a in arrays.items()}
    nc = bacc.Bacc("TRN2", target_bir_lowering=False, num_devices=1)
    args = [nc.dram_tensor(name, list(a.shape), mybir.dt.from_np(a.dtype), kind="ExternalInput").ap() for name, a in arrays.items()]
    out = nc.dram_tensor("out", [B, C, HH * WW], mybir.dt.float32, kind="ExternalOutput").ap()
    displaced_attention_kernel(nc, *args, out)
    result = run_bass_kernel_spmd(nc, [arrays], core_ids=[0]).results[0]["out"]
    return result.reshape(B, C, HH, WW)
```

```python
import concourse.bass as bass
from concourse import mybir
from contextlib import ExitStack

W_UP = 64.0


def group_scales_and_tables(nc, x, to_groups, from_groups, mean_rstd, offset, difference, taps_dram, weights, wh, wl):
    f32 = mybir.dt.float32
    ALU, ACT, AX = mybir.AluOpType, mybir.ActivationFunctionType, mybir.AxisListType
    P, SIZE = offset.shape[0], difference.shape[0]
    REACH, SIGMA = 2, 0.5
    SHARP = -1.0 / (2.0 * SIGMA ** 2)
    MAGIC = 1.5 * 2.0 ** 23
    MASK_AT = [3, 7]
    BATCH, C, PIX = x.shape[0], x.shape[1], x.shape[2]
    LANES, EPS, STAT = 128, 1e-5, 512
    CT = C // LANES
    NG = to_groups.shape[2]
    PIECE = PIX // 2
    LOADS = BATCH * CT * 2
    BUFS = 4
    PER = PIECE // STAT

    with ExitStack() as ctx:
        def sb(name, shape):
            return ctx.enter_context(nc.sbuf_tensor(name, shape, f32))

        def sem(name):
            return ctx.enter_context(nc.semaphore(name))

        off = sb("off", [SIZE, P, 2])
        diff = sb("diff", [SIZE, SIZE])
        whole, rest = sb("whole", [SIZE, 2, P]), sb("rest", [SIZE, 2, P])
        place, inside, norm = sb("place", [SIZE, 2, P]), sb("inside", [SIZE, 2, P]), sb("norm", [SIZE, 2, P])
        five = sb("five", [SIZE, 2, P, 2 * REACH + 1])
        dist, bell, near = sb("dist", [SIZE, P, SIZE]), sb("bell", [SIZE, P, SIZE]), sb("near", [SIZE, P, SIZE])
        pieces = sb("pieces", [LANES, BUFS, PIECE])
        w_stage = sb("w_stage", [LANES, CT, wh.shape[2]])
        stats = sb("gn_stats", [LANES, CT, BATCH, 2 * PER * 6])
        mean_sq = sb("mean_sq", [LANES, CT, BATCH, 2])
        square = sb("gn_square", [LANES, CT, BATCH])
        to_g = sb("to_g", [LANES, CT, NG])
        from_g = sb("from_g", [NG, C])
        group = sb("group", [NG, BATCH, 2])
        gsq = sb("gsq", [NG, BATCH])
        newton = sb("newton", [NG, BATCH])
        g_ps = ctx.enter_context(nc.psum_tensor("g_ps", [LANES, 512], f32))
        b_ps = ctx.enter_context(nc.psum_tensor("b_ps", [LANES, 512], f32))
        piece_in = [sem(f"piece_in{i}") for i in range(BUFS)]
        const_in, stat_done, step = sem("const_in"), sem("stat_done"), sem("gn_step")
        grouped, spread, rooted, summed = sem("grouped"), sem("spread"), sem("rooted"), sem("summed")
        off_in, off_split, five_set, five_exp = sem("off_in"), sem("off_split"), sem("five_set"), sem("five_exp")
        dist_set, bell_set, squared, bell_done = sem("dist_set"), sem("bell_set"), sem("squared"), sem("bell_done")
        masked, tap_done, taps_saved = sem("masked"), sem("tap_done"), sem("taps_saved")
        near_squared = sem("near_squared")
        w_in, w_hi_set, w_scaled, w_set = sem("w_in"), sem("w_hi_set"), sem("w_scaled"), sem("w_set")
        block = ctx.enter_context(nc.Block())

        @block.sync
        def _(sp):
            sp.dma_start(off[:, :, :], offset.unsqueeze(0).broadcast_to([SIZE, P, 2])).then_inc(off_in, 16)
            sp.dma_start(diff[:, :], difference).then_inc(off_in, 16)
            sp.dma_start(to_g[:, :, :], to_groups).then_inc(const_in, 16)
            sp.dma_start(from_g[:, :], from_groups).then_inc(const_in, 16)
            for n in range(LOADS):
                b, ct, half = n // (2 * CT), n // 2 % CT, n % 2
                if n >= BUFS:
                    sp.wait_ge(stat_done, PER * (n - BUFS + 1))
                sp.dma_start(pieces[:, n % BUFS, :], x[b, ct * LANES:(ct + 1) * LANES, half * PIECE:(half + 1) * PIECE])\
                  .then_inc(piece_in[n % BUFS], 16)
            col = 0
            for w in weights:
                sp.dma_start(w_stage[:, :, col:col + w.shape[1]], w.rearrange("(t p) n -> p t n", p=LANES)).then_inc(w_in, 16)
                col += w.shape[1]
            sp.wait_ge(taps_saved, 32)

        def wide(ap):
            return ap.unsqueeze(2).broadcast_to([SIZE, P, SIZE])

        @block.gpsimd
        def _(pool):
            pool.wait_ge(off_split, 1)
            for axis in range(2):
                if axis:
                    pool.wait_ge(masked, axis)
                nc.gpsimd.tensor_tensor(dist[:, :, :], diff[:, :].unsqueeze(1).broadcast_to([SIZE, P, SIZE]),
                                        wide(whole[:, axis, :]), ALU.add).then_inc(dist_set, 1)
                pool.wait_ge(dist_set, axis + 1)
                if axis:
                    pool.wait_ge(taps_saved, 16)
                nc.gpsimd.tensor_tensor(bell[:, :, :], dist[:, :, :], wide(rest[:, axis, :]), ALU.add).then_inc(bell_set, 1)
                pool.wait_ge(bell_done, axis + 1)
                pool.wait_ge(masked, axis + 1)
                nc.gpsimd.tensor_tensor(bell[:, :, :], bell[:, :, :], near[:, :, :], ALU.mult).then_inc(tap_done, 1)
            pool.wait_ge(w_hi_set, 1)
            pool.wait_ge(w_scaled, 1)
            nc.gpsimd.tensor_tensor(wl[:, :, :], w_stage[:, :, :], wh[:, :, :], ALU.subtract).then_inc(w_set, 1)
            pool.wait_ge(w_set, 1)

        @block.vector
        def _(dve):
            count = [0]

            def split_offsets():
                v = nc.vector
                dve.wait_ge(off_in, 32)
                o = off[:, :, :].rearrange("m p a -> m a p")
                link(v.tensor_scalar(whole[:, :, :], o, MAGIC, None, ALU.add))
                link(v.tensor_scalar(whole[:, :, :], whole[:, :, :], MAGIC, None, ALU.subtract))
                v.tensor_tensor(rest[:, :, :], o, whole[:, :, :], ALU.subtract).then_inc(off_split, 1)
                dve.wait_ge(off_split, 1)
                for u in range(2 * REACH + 1):
                    link(v.tensor_scalar(five[:, :, :, u], rest[:, :, :], float(u - REACH), None, ALU.add))
                v.tensor_tensor(five[:, :, :, :], five[:, :, :, :], five[:, :, :, :], ALU.mult).then_inc(five_set, 1)
                link(v.tensor_scalar(place[:, :, :], whole[:, :, :], diff[:, 0:1], None, ALU.add))
                link(v.tensor_scalar(inside[:, :, :], place[:, :, :], 0.0, None, ALU.is_ge))
                link(v.tensor_scalar(place[:, :, :], place[:, :, :], float(SIZE - 1), None, ALU.is_le))
                link(v.tensor_tensor(inside[:, :, :], inside[:, :, :], place[:, :, :], ALU.mult))
                dve.wait_ge(five_exp, 1)
                link(v.tensor_reduce(norm[:, :, :], five[:, :, :, :], AX.X, ALU.add))
                link(v.reciprocal(norm[:, :, :], norm[:, :, :]))
                link(v.tensor_tensor(norm[:, :, :], norm[:, :, :], inside[:, :, :], ALU.mult))

            def mask(axis):
                dve.wait_ge(near_squared, axis + 1)
                link(nc.vector.tensor_scalar(near[:, :, :], near[:, :, :], (REACH + 0.5) ** 2, None, ALU.is_le))
                nc.vector.tensor_tensor(near[:, :, :], near[:, :, :], wide(norm[:, axis, :]), ALU.mult).then_inc(masked, 1)

            def link(ins):
                count[0] += 1
                ins.then_inc(step, 1)
                dve.wait_ge(step, count[0])

            split_offsets()
            for n in range(LOADS):
                b, ct, half = n // (2 * CT), n // 2 % CT, n % 2
                if n in MASK_AT:
                    mask(MASK_AT.index(n))
                dve.wait_ge(piece_in[n % BUFS], 16 * (n // BUFS + 1))
                for i in range(PER):
                    at = (half * PER + i) * 6
                    nc.vector.bn_stats(stats[:, ct, b, at:at + 6], pieces[:, n % BUFS, i * STAT:(i + 1) * STAT])\
                      .then_inc(stat_done, 1)
            dve.wait_ge(stat_done, LOADS * PER)
            for ct in range(CT):
                for b in range(BATCH):
                    last = nc.vector.bn_aggr(mean_sq[:, ct, b, :], stats[:, ct, b, :])
                    if (ct, b) != (CT - 1, BATCH - 1):
                        link(last)
            link(last)
            link(nc.vector.tensor_tensor(square[:, :, :], mean_sq[:, :, :, 0], mean_sq[:, :, :, 0], ALU.mult))
            nc.vector.tensor_tensor(mean_sq[:, :, :, 1], mean_sq[:, :, :, 1], square[:, :, :], ALU.add).then_inc(summed, 1)
            dve.wait_ge(grouped, 1)
            link(nc.vector.tensor_copy(group[:, :, :], g_ps[0:NG, 0:2 * BATCH].rearrange("p (b k) -> p b k", k=2)))
            link(nc.vector.tensor_tensor(gsq[:, :], group[:, :, 0], group[:, :, 0], ALU.mult))
            link(nc.vector.tensor_tensor(group[:, :, 1], group[:, :, 1], gsq[:, :], ALU.subtract))
            nc.vector.tensor_scalar(group[:, :, 1], group[:, :, 1], EPS, None, ALU.add).then_inc(summed, 1)
            dve.wait_ge(rooted, 1)
            link(nc.vector.reciprocal(gsq[:, :], gsq[:, :]))
            link(nc.vector.tensor_tensor(newton[:, :], gsq[:, :], gsq[:, :], ALU.mult))
            link(nc.vector.tensor_tensor(newton[:, :], newton[:, :], group[:, :, 1], ALU.mult))
            link(nc.vector.tensor_scalar(newton[:, :], newton[:, :], -0.5, 1.5, ALU.mult, ALU.add))
            nc.vector.tensor_tensor(group[:, :, 1], gsq[:, :], newton[:, :], ALU.mult).then_inc(summed, 1)
            dve.wait_ge(spread, 1)
            link(nc.vector.tensor_copy(mean_rstd[:, :, :, :],
                                       b_ps[:, 0:CT * BATCH * 2].rearrange("p (t b k) -> p t b k", b=BATCH, k=2)))

        @block.scalar
        def _(act):
            act.wait_ge(five_set, 1)
            nc.scalar.activation(five[:, :, :, :], five[:, :, :, :], ACT.Exp, scale=SHARP).then_inc(five_exp, 1)
            for axis in range(2):
                act.wait_ge(dist_set, axis + 1)
                nc.scalar.activation(near[:, :, :], dist[:, :, :], ACT.Square).then_inc(near_squared, 1)
                act.wait_ge(bell_set, axis + 1)
                nc.scalar.activation(bell[:, :, :], bell[:, :, :], ACT.Square).then_inc(squared, 1)
                act.wait_ge(squared, axis + 1)
                nc.scalar.activation(bell[:, :, :], bell[:, :, :], ACT.Exp, scale=SHARP).then_inc(bell_done, 1)
                act.wait_ge(tap_done, axis + 1)
                act.dma_start(taps_dram[:, axis, :, :], bell[:, :, :]).then_inc(taps_saved, 16)
            act.wait_ge(w_in, 16 * len(weights))
            nc.scalar.mul(wh[:, :, :], w_stage[:, :, :], W_UP).then_inc(w_hi_set, 1)
            act.wait_ge(w_hi_set, 1)
            nc.scalar.mul(w_stage[:, :, :], w_stage[:, :, :], W_UP).then_inc(w_scaled, 1)
            act.wait_ge(summed, 2)
            nc.scalar.activation(gsq[:, :], group[:, :, 1], ACT.Sqrt).then_inc(rooted, 1)

        @block.tensor
        def _(pe):
            pe.wait_ge(const_in, 32)
            pe.wait_ge(summed, 1)
            for ct in range(CT):
                last = nc.tensor.matmul(g_ps[0:NG, 0:2 * BATCH], to_g[:, ct, :],
                                        mean_sq[:, ct, :, :].rearrange("p b k -> p (b k)"), start=ct == 0, stop=ct == CT - 1)
            last.then_inc(grouped, 1)
            pe.wait_ge(summed, 3)
            for ct in range(CT):
                last = nc.tensor.matmul(b_ps[:, ct * 2 * BATCH:(ct + 1) * 2 * BATCH], from_g[:, ct * LANES:(ct + 1) * LANES],
                                        group[:, :, :].rearrange("p b k -> p (b k)"), start=True, stop=True)
            last.then_inc(spread, 1)


def project_and_window_attention(nc, x, wh, wl, ident_dram, mean_rstd,
                                 q_dram, k_dram, v_dram, win_dram):
    f32, f16 = mybir.dt.float32, mybir.dt.float16
    ALU, ACT, AX = mybir.AluOpType, mybir.ActivationFunctionType, mybir.AxisListType
    BATCH, C = x.shape[0], x.shape[1]
    LANES, D, H, WN, IMW = 128, 32, 6, 4, 96
    CT = C // LANES
    CHUNKS = q_dram.shape[1]
    N = BATCH * CHUNKS
    TOK = x.shape[2] // CHUNKS
    WIN = TOK // WN
    WT = WIN // LANES
    HD = H * D
    M = 3 * D
    QKV, LQ, LKV = 0, 3 * HD, 4 * HD
    SCALE = float(D) ** -0.5
    MEAN = 1 / W_UP / WN
    BANK = 512
    AHEAD = [(0, 1), (2,), ()]
    HIGH_AT = 5
    POOLED_AT = 6
    TRANSPOSE_AT = (7, 8)
    UNITS, RING = 28, 7

    with ExitStack() as ctx:
        def sb(name, shape, dt=f32):
            return ctx.enter_context(nc.sbuf_tensor(name, shape, dt))

        def sem(name):
            return ctx.enter_context(nc.semaphore(name))

        x_in_sb = sb("x_in_sb", [LANES, 2, CT, TOK])
        xn = sb("xn", [LANES, CT, TOK])
        xh, xl = sb("xh", [LANES, 2 * CT * TOK], f16), sb("xl", [LANES, 2 * CT * TOK], f16)
        pool4 = sb("pool4", [LANES, CT, WIN])
        ph, pl = sb("ph", [LANES, CT, WIN], f16), sb("pl", [LANES, CT, WIN], f16)
        ident = sb("ident", [LANES, LANES])
        qkv = sb("qkv", [LANES, WT, WN, 3 * HD])
        prod_s = sb("prod_s", [LANES, WN * WN, HD])
        prod_v = sb("prod_v", [LANES, WN, WN, HD])
        scores = sb("scores", [LANES, WN, WN, H])
        win_max, win_sum = sb("win_max", [LANES, WN, H]), sb("win_sum", [LANES, WN, H])
        probs_e = sb("probs_e", [LANES, WN, WN, H])
        probs_w = sb("probs_w", [LANES, WN, WN, H])
        win_out = sb("win_out", [LANES, WN, HD])
        win_t = sb("win_t", [M, 2, BANK])
        q_st = sb("q_st", [M, 2, 2, TOK], f16)
        k_st = sb("k_st", [M, 2, 2, WIN], f16)
        v_st = sb("v_st", [LANES, WT, HD])
        ring_ps = ctx.enter_context(nc.psum_tensor("ring_ps", [LANES, RING, BANK], f32))
        t_ps = ctx.enter_context(nc.psum_tensor("t_ps", [LANES, BANK], f32))

        ident_in = sem("ident_in")
        x_loaded, xn_done, xh_done, xl_done = sem("x_loaded"), sem("xn_done"), sem("xh_done"), sem("xl_done")
        summed, ph_done, pl_done = sem("pool_summed"), sem("ph_done"), sem("pl_done")
        unit_done, act_evac, dve_evac = sem("unit_done"), sem("act_evac"), sem("dve_evac")
        hi_step, sub_done, exp_done_w, probs_done = sem("hi_step"), sem("sub_done"), sem("exp_done_w"), sem("probs_done")
        prod_v_done, win_done, t_done, t_evac = sem("prod_v_done"), sem("win_done"), sem("t_done"), sem("t_evac")
        q_saved, kv_saved, win_saved = sem("q_saved"), sem("kv_saved"), sem("win_saved")
        block = ctx.enter_context(nc.Block())

        units = []
        for wt in range(WT):
            units += [("qk", wt, i) for i in range(WN)] + [("v", wt, i) for i in range(2)]
            if wt < 2:
                units += [("lq", wt, i) for i in range(3)]
            else:
                units += [("lk", wt, i) for i in range(2)] + [("lv", wt, i) for i in range(2)]
        assert len(units) == UNITS and UNITS % RING == 0
        DVE_UNITS = [n for n, u in enumerate(units) if u[0] in ("lq", "lk")]
        ND = len(DVE_UNITS)

        def half(buf, s):
            return buf[:, bass.ds(s % 2 * (CT * TOK), CT * TOK)].rearrange("p (t i w) -> p t i w", t=CT, i=WN)

        @block.sync
        def _(sp):
            def load_x(s):
                if not isinstance(s, int) or s > 0:
                    sp.wait_ge(x_loaded, 48 * s)
                src = x[bass.ds(s // CHUNKS, 1), :, bass.ds(s % CHUNKS * TOK, TOK)][0]
                for ct in range(CT):
                    dst = x_in_sb[:, :, :, :].rearrange("p a t n -> p (a t n)")[:, bass.ds(s % 2 * (CT * TOK) + ct * TOK, TOK)]
                    sp.dma_start(dst, src[ct * LANES:(ct + 1) * LANES, :]).then_inc(x_loaded, 16)

            def save_window(turn):
                sp.wait_ge(t_evac, 2 * (turn + 2))
                for kt in range(2):
                    sp.dma_start(win_dram[bass.ds(turn, 1)][0, kt], win_t[:, kt, :]).then_inc(win_saved, 16)

            def save_chunk(s):
                b, c = s // CHUNKS, s % CHUNKS
                for wt in range(WT):
                    save_window(WT * s + wt)
                    if wt < 2:
                        sp.wait_ge(dve_evac, ND * (s + 1) + 3 * (wt + 1))
                        for part in range(2):
                            dst = q_dram[bass.ds(b, 1), bass.ds(c, 1), part, wt * 3:wt * 3 + 3][0, 0].rearrange("h d n -> (h d) n")
                            sp.dma_start(dst, q_st[:, wt, part, :]).then_inc(q_saved, 16)
                    else:
                        sp.wait_ge(dve_evac, ND * (s + 1) + ND)
                        for mt in range(2):
                            for part in range(2):
                                dst = k_dram[bass.ds(b, 1), part, mt * 3:mt * 3 + 3, :, bass.ds(c * WIN, WIN)][0]
                                sp.dma_start(dst.rearrange("h d n -> (h d) n"), k_st[:, mt, part, :]).then_inc(kv_saved, 16)
                        sp.wait_ge(act_evac, UNITS * (s + 1) + RING)
                        for w in range(WT):
                            dst = v_dram[bass.ds(b, 1), :, :, bass.ds(c * WT * D + w * D, D)][0].rearrange("h p d -> p h d")
                            sp.dma_start(dst, v_st[:, w, :].rearrange("p (h d) -> p h d", d=D)).then_inc(kv_saved, 16)

            load_x(0)
            sp.dma_start(ident[:, :], ident_dram).then_inc(ident_in, 16)
            load_x(1)
            with sp.Fori(0, N - 2) as s:
                sp.wait_ge(xn_done, CT * (s + 1))
                load_x(s + 2)
                save_chunk(s)
            with sp.Fori(N - 2, N) as s:
                save_chunk(s)
            save_window(WT * N)
            save_window(WT * N + 1)
            sp.wait_ge(win_saved, 32 * (WT * N + 3))
            sp.wait_ge(q_saved, 64 * (N + 1))
            sp.wait_ge(kv_saved, 112 * (N + 1))

        @block.tensor
        def _(pe):
            def unit(s, n):
                kind, wt, i = units[n]
                pe.wait_ge(act_evac, UNITS * s + n + 1)
                old = (n - RING) % UNITS
                if old in DVE_UNITS:
                    pe.wait_ge(dve_evac, ND * (s + (n >= RING)) + DVE_UNITS.index(old) + 1)
                bank = n % RING
                h, l = half(xh, s), half(xl, s)
                hh, hl, lh = (0, 0), (0, 1), (1, 0)
                if kind in ("qk", "v"):
                    runs = [(i, 0, QKV, 2 * HD)] if kind == "qk" else [(2 * i, 0, QKV + 2 * HD, HD), (2 * i + 1, HD, QKV + 2 * HD, HD)]
                    for place, to, col, width in runs:
                        terms = [(ct, a, b) for ct in range(CT) for a, b in (hh, hl, lh)]
                        for m, (ct, a, b) in enumerate(terms):
                            last = nc.tensor.matmul(ring_ps[:, bank, to:to + width],
                                                    (h, l)[a][:, ct, place, wt * LANES:(wt + 1) * LANES],
                                                    (wh, wl)[b][:, ct, col:col + width], start=m == 0, stop=m == len(terms) - 1)
                elif kind == "lv":
                    for w in ((0, 1), (2,))[i]:
                        terms = [(ct, a, b) for ct in range(CT) for a, b in (hh, hl, lh)]
                        for m, (ct, a, b) in enumerate(terms):
                            last = nc.tensor.matmul(ring_ps[:, bank, w % 2 * HD:w % 2 * HD + HD],
                                                    (ph, pl)[a][:, ct, w * LANES:(w + 1) * LANES],
                                                    (wh, wl)[b][:, ct, LKV + HD:LKV + 2 * HD], start=m == 0, stop=m == len(terms) - 1)
                else:
                    terms = [(ct, a, b) for ct in range(CT) for a, b in (hh, hl, lh)]
                    for m, (ct, a, b) in enumerate(terms):
                        if kind == "lq":
                            col = LQ + wt * M
                            moving = (h, l)[b][:, ct].rearrange("p i w -> p (i w)")[:, i * BANK:(i + 1) * BANK]
                        else:
                            col = LKV + i * M
                            moving = (ph, pl)[b][:, ct, :]
                        width = BANK if kind == "lq" else WIN
                        last = nc.tensor.matmul(ring_ps[0:M, bank, 0:width], (wh, wl)[a][:, ct, col:col + M], moving,
                                                start=m == 0, stop=m == len(terms) - 1)
                last.then_inc(unit_done, 1)

            def transposes(turn, kt):
                pe.wait_ge(win_done, turn + 1)
                pe.wait_ge(t_evac, 2 * turn + kt + 2)
                for i in range(WN):
                    last = nc.tensor.transpose(t_ps[0:M, i * LANES:(i + 1) * LANES], win_out[:, i, kt * M:(kt + 1) * M], ident[:, :])
                last.then_inc(t_done, 1)

            pe.wait_ge(ident_in, 16)
            pe.sem_inc(unit_done, UNITS)
            pe.sem_inc(t_done, 2)
            with pe.Fori(0, N) as s:
                pe.wait_ge(xh_done, CT * (s + 2))
                pe.wait_ge(xl_done, CT * (s + 2))
                for wt in range(WT):
                    mine = [n for n in range(UNITS) if units[n][1] == wt]
                    for at, n in enumerate(mine):
                        if units[n][0] == "lk":
                            pe.wait_ge(ph_done, s + 1)
                            pe.wait_ge(pl_done, s + 1)
                        unit(s, n)
                        if at in TRANSPOSE_AT:
                            transposes(WT * s + wt, TRANSPOSE_AT.index(at))
            for turn in (WT * N, WT * N + 1):
                for kt in range(2):
                    transposes(turn, kt)

        @block.scalar
        def _(act):
            def evac(s, n):
                kind, wt, i = units[n]
                act.wait_ge(unit_done, UNITS * (s + 1) + n + 1)
                src = ring_ps[:, n % RING, :]
                if kind == "qk":
                    if i == 0:
                        act.wait_ge(prod_v_done, WT * s + wt + 1)
                    ins = nc.scalar.mul(qkv[:, wt, i, 0:2 * HD], src[:, 0:2 * HD], 1 / W_UP)
                elif kind == "v":
                    ins = nc.scalar.mul(qkv[:, wt, 2 * i:2 * i + 2, 2 * HD:3 * HD], src[:, 0:2 * HD].rearrange("p (a n) -> p a n", a=2), 1 / W_UP)
                elif kind == "lq":
                    act.wait_ge(q_saved, 64 * (s + 1))
                    ins = nc.scalar.mul(q_st[:, wt, 0, i * BANK:(i + 1) * BANK], src[0:M, :], 1 / W_UP)
                elif kind == "lk":
                    act.wait_ge(kv_saved, 112 * (s + 1))
                    ins = nc.scalar.mul(k_st[:, i, 0, :], src[0:M, 0:WIN], MEAN)
                elif i == 0:
                    ins = nc.scalar.mul(v_st[:, 0:2, :], src[:, 0:2 * HD].rearrange("p (a n) -> p a n", a=2), MEAN)
                else:
                    ins = nc.scalar.mul(v_st[:, 2, :], src[:, 0:HD], MEAN)
                ins.then_inc(act_evac, 1)

            def high_part(u, ct):
                act.wait_ge(xn_done, CT * u + ct + 1)
                if not isinstance(u, int):
                    act.wait_ge(unit_done, UNITS * u)
                nc.scalar.copy(half(xh, u)[:, ct], xn[:, ct, :].rearrange("p (i w) -> p i w", i=WN)).then_inc(xh_done, 1)

            def t_out(turn, kt):
                act.wait_ge(t_done, 2 * (turn + 1) + kt + 1)
                if kt == 0:
                    act.wait_ge(win_saved, 32 * (turn + 1))
                nc.scalar.copy(win_t[:, kt, :], t_ps[0:M, :]).then_inc(t_evac, 1)

            def pooled_high(s):
                act.wait_ge(summed, CT * (WN - 1) * (s + 2))
                act.wait_ge(unit_done, UNITS * (s + 1))
                nc.scalar.copy(ph[:, :, :], pool4[:, :, :]).then_inc(ph_done, 1)

            def turn(s, wt, ahead):
                mine = [n for n in range(UNITS) if units[n][1] == wt]
                for at, n in enumerate(mine):
                    evac(s, n)
                    if at == HIGH_AT and ahead and wt > 0:
                        for ct in AHEAD[wt - 1]:
                            high_part(s + 1, ct)
                    if at in TRANSPOSE_AT:
                        t_out(WT * s + wt, TRANSPOSE_AT.index(at))
                    if at == POOLED_AT and wt == 0:
                        pooled_high(s)
                act.wait_ge(sub_done, WT * s + wt + 1)
                nc.scalar.activation(probs_e[:, :, :, :], scores[:, :, :, :], ACT.Exp, scale=SCALE).then_inc(exp_done_w, 1)

            act.sem_inc(act_evac, RING)
            act.sem_inc(t_evac, 2)
            act.sem_inc(xh_done, CT)
            act.sem_inc(win_saved, 32)
            act.sem_inc(q_saved, 64)
            act.sem_inc(kv_saved, 112)
            for ct in range(CT):
                high_part(0, ct)
            with act.Fori(0, N - 1) as s:
                for wt in range(WT):
                    turn(s, wt, True)
            for wt in range(WT):
                turn(N - 1, wt, False)
            for last_turn in (WT * N, WT * N + 1):
                for kt in range(2):
                    t_out(last_turn, kt)

        @block.gpsimd
        def _(pool):
            def low_part(u, ct):
                pool.wait_ge(xh_done, CT * (u + 1) + ct + 1)
                view = xn[:, ct, :].rearrange("p (i w) -> p i w", i=WN)
                nc.gpsimd.tensor_tensor(half(xl, u)[:, ct], view, half(xh, u)[:, ct], ALU.subtract).then_inc(xl_done, 1)

            def window_sums(u, ct):
                base = (WN - 1) * (CT * u + ct)
                view = xn[:, ct, :].rearrange("p (i w) -> p i w", i=WN)
                for i in range(1, WN):
                    if i == 1:
                        if not isinstance(u, int):
                            pool.wait_ge(pl_done, u)
                    else:
                        pool.wait_ge(summed, base + i + CT * (WN - 1) - 1)
                    first = view[:, 0] if i == 1 else pool4[:, ct, :]
                    nc.gpsimd.tensor_tensor(pool4[:, ct, :], first, view[:, i], ALU.add).then_inc(summed, 1)

            def pooled_low(s):
                pool.wait_ge(ph_done, s + 1)
                nc.gpsimd.tensor_tensor(pl[:, :, :], pool4[:, :, :], ph[:, :, :], ALU.subtract).then_inc(pl_done, 1)

            def windows(s, wt):
                pool.wait_ge(probs_done, WT * s + wt + 1)
                for i in range(WN):
                    p = probs_w[:, i, :, :].unsqueeze(3).broadcast_to([LANES, WN, H, D])
                    v = qkv[:, wt, :, 2 * HD:3 * HD].rearrange("p j (h d) -> p j h d", d=D)
                    last = nc.gpsimd.tensor_tensor(prod_v[:, i, :, :].rearrange("p j (h d) -> p j h d", d=D), p, v, ALU.mult)
                last.then_inc(prod_v_done, 1)

            nc.gpsimd.memset(prod_v[:, :, :, :].rearrange("p a b c -> p (a b c)"), 0.0).then_inc(prod_v_done, 1)
            pool.sem_inc(prod_v_done, WT - 1)
            pool.sem_inc(xl_done, CT)
            pool.sem_inc(summed, CT * (WN - 1))
            for ct in range(CT):
                low_part(0, ct)
            for ct in range(CT):
                window_sums(0, ct)

            def turns(s, ahead):
                pooled_low(s)
                for wt in range(WT):
                    windows(s, wt)
                    if ahead and wt == 0:
                        for ct in range(CT):
                            low_part(s + 1, ct)
                            window_sums(s + 1, ct)

            with pool.Fori(0, N - 1) as s:
                turns(s, True)
            turns(N - 1, False)

        @block.vector
        def _(dve):
            SMALL = 5
            def normalise(u, ct):
                dve.wait_ge(x_loaded, 48 * (u + 1))
                dve.wait_ge(xh_done, CT * u + ct + 1)
                dve.wait_ge(xl_done, CT * u + ct + 1)
                dve.wait_ge(summed, (WN - 1) * (CT * u + ct + 1))
                b = u // CHUNKS
                flat = x_in_sb[:, :, :, :].rearrange("p a t n -> p (a t n)")
                src = flat[:, bass.ds(u % 2 * (CT * TOK) + ct * TOK, TOK)].rearrange(
                    "p (wy dy wx dx) -> p dy dx wy wx", dy=2, dx=2, wx=IMW // 2)
                dst = xn[:, ct, :].rearrange("p (dy dx wy wx) -> p dy dx wy wx", dy=2, dx=2, wx=IMW // 2)
                scal = mean_rstd[:, :, :, :].rearrange("p t b k -> p (t b k)")
                mean, rstd = (scal[:, bass.ds(ct * 2 * BATCH + b * 2 + k, 1)] for k in range(2))
                for dy in range(2):
                    last = nc.vector.tensor_scalar(dst[:, dy], src[:, dy], mean, rstd, ALU.subtract, ALU.mult)
                last.then_inc(xn_done, 1)

            def low_evac(s, n):
                kind, wt, i = units[n]
                dve.wait_ge(act_evac, UNITS * s + n + 1 + RING)
                if kind == "lq":
                    at = slice(i * BANK, (i + 1) * BANK)
                    ins = nc.vector.scalar_tensor_tensor(q_st[:, wt, 1, at], ring_ps[0:M, n % RING, :], 1 / W_UP, q_st[:, wt, 0, at],
                                                         ALU.mult, ALU.subtract)
                else:
                    ins = nc.vector.scalar_tensor_tensor(k_st[:, i, 1, :], ring_ps[0:M, n % RING, 0:WIN], MEAN, k_st[:, i, 0, :],
                                                         ALU.mult, ALU.subtract)
                ins.then_inc(dve_evac, 1)

            def finish(turn):
                dve.wait_ge(prod_v_done, turn + WT)
                dve.wait_ge(t_done, 2 * (turn + 2))
                nc.vector.tensor_reduce(win_out[:, :, :], prod_v[:, :, :, :].rearrange("p i j n -> p i n j"), AX.X, ALU.add).then_inc(win_done, 1)

            def windows(s, wt, ahead):
                turn = WT * s + wt
                n_hi = max(n for n in range(UNITS) if units[n][1] == wt and units[n][0] == "v")
                dve.wait_ge(act_evac, UNITS * s + n_hi + 1 + RING)
                q = qkv[:, wt, :, 0:HD].unsqueeze(2).broadcast_to([LANES, WN, WN, HD])
                k = qkv[:, wt, :, HD:2 * HD].unsqueeze(1).broadcast_to([LANES, WN, WN, HD])
                base = SMALL * turn
                nc.vector.tensor_tensor(prod_s[:, :, :].rearrange("p (i j) n -> p i j n", j=WN), q, k, ALU.mult).then_inc(hi_step, 1)
                dve.wait_ge(hi_step, base + 1)
                nc.vector.tensor_reduce(scores[:, :, :, :].rearrange("p i j h -> p (i j h)"),
                                        prod_s[:, :, :].rearrange("p a (h d) -> p (a h) d", d=D), AX.X, ALU.add).then_inc(hi_step, 1)
                dve.wait_ge(hi_step, base + 2)
                nc.vector.tensor_reduce(win_max[:, :, :], scores[:, :, :, :].rearrange("p i j h -> p i h j"), AX.X, ALU.max).then_inc(hi_step, 1)
                dve.wait_ge(hi_step, base + 3)
                nc.vector.tensor_tensor(scores[:, :, :, :], scores[:, :, :, :],
                                        win_max[:, :, :].unsqueeze(2).broadcast_to([LANES, WN, WN, H]), ALU.subtract).then_inc(sub_done, 1)
                for n in DVE_UNITS:
                    if units[n][1] == wt:
                        low_evac(s, n)
                finish(turn)
                dve.wait_ge(exp_done_w, turn + 1)
                nc.vector.tensor_reduce(win_sum[:, :, :], probs_e[:, :, :, :].rearrange("p i j h -> p i h j"), AX.X, ALU.add).then_inc(hi_step, 1)
                dve.wait_ge(hi_step, base + 4)
                nc.vector.reciprocal(win_sum[:, :, :], win_sum[:, :, :]).then_inc(hi_step, 1)
                dve.wait_ge(hi_step, base + 5)
                nc.vector.tensor_tensor(probs_w[:, :, :, :], probs_e[:, :, :, :],
                                        win_sum[:, :, :].unsqueeze(2).broadcast_to([LANES, WN, WN, H]), ALU.mult).then_inc(probs_done, 1)
                if ahead:
                    for ct in AHEAD[wt]:
                        normalise(s + 1, ct)

            nc.vector.memset(win_out[:, :, :], 0.0).then_inc(win_done, 1)
            dve.sem_inc(dve_evac, ND)
            for ct in range(CT):
                normalise(0, ct)
            with dve.Fori(0, N - 1) as s:
                for wt in range(WT):
                    windows(s, wt, True)
            for wt in range(WT):
                windows(N - 1, wt, False)
            finish(WT * N)


def global_attention(nc, q_dram, k_dram, v_dram, m_dram, o_dram):
    f32, f16 = mybir.dt.float32, mybir.dt.float16
    ALU, ACT, AX = mybir.AluOpType, mybir.ActivationFunctionType, mybir.AxisListType
    BATCH, CHUNKS, D, QT = q_dram.shape[0], q_dram.shape[1], 32, q_dram.shape[5]
    HEADS, KEYS = q_dram.shape[3], k_dram.shape[4]
    LANES = 128
    GROUPS = BATCH * HEADS
    TILES = GROUPS * CHUNKS
    KB = KEYS // LANES
    QB = QT // LANES
    QUARTER = QT // 4
    BANK = 512
    UNITS = KB * QT // BANK
    CHUNK_UNITS = [2] * (UNITS // 2 - 1) + [1, 1]
    NCH = len(CHUNK_UNITS)
    CHUNK_START = [sum(CHUNK_UNITS[:k]) for k in range(NCH)]
    RING = 6
    SCALE = float(D) ** -0.5
    STEP = 64.0
    POOL_KB = [0, 1, 2, 4, 5, 7, 8, 10, 11, 13, 14, 15]
    ADDS = len(POOL_KB) - 1
    SUM_KB = [b for b in range(KB) if b not in POOL_KB]
    added = {b: max(n, 1) for n, b in enumerate(POOL_KB)}
    MAXU = QB * KEYS // BANK
    last_chunk = {b: max(k for k in range(NCH) if CHUNK_START[k] * BANK < (b + 1) * QT) for b in range(KB)}
    PV_LAG = 2
    LATE_KB = KB - 2
    LATE_AT = [1, 2]
    QK_LEN, PV_LEN = BANK, 4 * QUARTER
    TILE_LEN = UNITS * QK_LEN + (KB + len(SUM_KB) + 1) * PV_LEN
    PIECES = 4
    INVERT_AT = [13, 21, 29, 37]
    NORMALISE_AT = 7
    FOLD_AT = 2
    MOVE_AT = 2

    with ExitStack() as ctx:
        def sb(name, shape, dt):
            return ctx.enter_context(nc.sbuf_tensor(name, shape, dt))

        def sem(name):
            return ctx.enter_context(nc.semaphore(name))

        q_ring = sb("q_ring", [LANES, 4 * QT], f16)
        k_ring = sb("k_ring", [LANES, 2 * KEYS], f16)
        v_ring = sb("v_ring", [LANES, 2 * KB * D], f32)
        v_now = sb("v_now", [LANES, KB * D], f32)
        ones = sb("ones32", [LANES, D], f32)
        probs = sb("probs", [LANES, RING * QT], f32)
        prob_sum = sb("prob_sum", [LANES, QT], f32)
        part_max = sb("part_max", [LANES, QB, 5], f32)
        tile_max = sb("tile_max", [LANES, 32], f32)
        max_rows = sb("max_rows", [LANES, 32], f32)
        max_split = sb("max_split", [LANES, 2, 32], f16)
        out_sum = sb("out_sum", [LANES, 2, QUARTER], f32)
        recip = sb("recip", [LANES, QUARTER], f32)
        o_norm = sb("o_norm", [LANES, QUARTER], f32)
        score_ps = ctx.enter_context(nc.psum_tensor("score_ps", [LANES, 4, BANK], f32))
        max_ps = ctx.enter_context(nc.psum_tensor("max_ps", [LANES, 2, BANK], f32))
        out_ps = ctx.enter_context(nc.psum_tensor("out_ps", [LANES, BANK], f32))
        sum_ps = ctx.enter_context(nc.psum_tensor("sum_ps", [LANES, BANK], f32))

        q_in, kv_in, m_in, m_saved = sem("q_in"), sem("kv_in"), sem("m_in"), sem("m_saved")
        consts_set, v_set, qk_done, exp_done = sem("consts_set"), sem("v_set"), sem("qk_done"), sem("exp_done")
        pv_done, adds_done, fold_done = sem("pv_done"), sem("adds_done"), sem("fold_done")
        maxqk_done, max_read, m_ready, o_ready = sem("maxqk_done"), sem("max_read"), sem("m_ready"), sem("o_ready")
        o_saved, dve_step, out_moved, sum_moved = sem("o_saved"), sem("dve_step"), sem("out_moved"), sem("sum_moved")
        recip_done = sem("recip_done")
        block = ctx.enter_context(nc.Block())

        @block.sync
        def _(sp):
            def load_q(t):
                if not isinstance(t, int) or t > 0:
                    sp.wait_ge(q_in, 48 * t)
                src = q_dram[bass.ds((t // CHUNKS) // HEADS, 1), bass.ds(t % CHUNKS, 1), :, bass.ds((t // CHUNKS) % HEADS, 1)]
                for part, row in ((0, 0), (0, D), (1, 2 * D)):
                    sp.dma_start(q_ring[row:row + D, bass.ds(t % 4 * QT, QT)], src[0, 0, part, 0]).then_inc(q_in, 16)

            def load_kv(g):
                if not isinstance(g, int) or g > 0:
                    sp.wait_ge(kv_in, 64 * g)
                b, h = g // HEADS, g % HEADS
                src = k_dram[bass.ds(b, 1), :, bass.ds(h, 1)]
                for part, row in ((0, 0), (1, D), (0, 2 * D)):
                    sp.dma_start(k_ring[row:row + D, bass.ds(g % 2 * KEYS, KEYS)], src[0, part, 0]).then_inc(kv_in, 16)
                sp.dma_start(v_ring[:, bass.ds(g % 2 * KB * D, KB * D)], v_dram[bass.ds(b, 1), bass.ds(h, 1)][0, 0]).then_inc(kv_in, 16)

            def save_o(t):
                sp.wait_ge(o_ready, t + 2)
                dst = o_dram[bass.ds((t // CHUNKS) // HEADS, 1), bass.ds(t % CHUNKS, 1), bass.ds((t // CHUNKS) % HEADS * D, D)][0, 0]
                for quarter in range(4):
                    sp.dma_start(dst[:, quarter * QUARTER:(quarter + 1) * QUARTER],
                                 o_norm[quarter * D:(quarter + 1) * D, :]).then_inc(o_saved, 16)

            sp.sem_inc(o_saved, 64)
            load_kv(0)
            for t in range(3):
                load_q(t)
            with sp.Fori(0, GROUPS - 1) as g:
                for c in range(CHUNKS):
                    if c == 3:
                        load_kv(g + 1)
                    load_q(g * CHUNKS + c + 3)
                    save_o(g * CHUNKS + c)
            for c in range(CHUNKS):
                t = (GROUPS - 1) * CHUNKS + c
                if c < 3:
                    load_q(t + 3)
                save_o(t)
            sp.wait_ge(o_saved, 64 * (TILES + 1))

        @block.tensor
        def _(pe):
            def max_unit(t, j):
                pair, r = j // 9, j % 9
                pe.wait_ge(max_read, MAXU * t + j + 1)
                keys = t // CHUNKS % 2 * KEYS
                if r < 8:
                    parts = [(2 * pair + r // 4, (r % 4) * BANK, 0, BANK)]
                else:
                    parts = [(2 * pair, 4 * BANK, 0, KEYS - 4 * BANK), (2 * pair + 1, 4 * BANK, 256, KEYS - 4 * BANK)]
                for qb, at, to, n in parts:
                    last = nc.tensor.matmul(max_ps[:, j % 2, to:to + n], q_ring[0:3 * D, bass.ds(t % 4 * QT + qb * LANES, LANES)],
                                            k_ring[0:3 * D, bass.ds(keys + at, n)], start=True, stop=True)
                last.then_inc(maxqk_done, 1)

            def qk_chunk(t, k):
                pe.wait_ge(exp_done, NCH * t + k + 1)
                for i in range(CHUNK_UNITS[k]):
                    u = CHUNK_START[k] + i
                    kb, at = u * BANK // QT, u * BANK % QT
                    last = nc.tensor.matmul(score_ps[:, k % 2 * 2 + i, :],
                                            k_ring[0:3 * D + 2, bass.ds(t // CHUNKS % 2 * KEYS + kb * LANES, LANES)],
                                            q_ring[0:3 * D + 2, bass.ds(t % 4 * QT + at, BANK)], start=True, stop=True)
                last.then_inc(qk_done, 1)

            def pv(t, kb):
                pe.wait_ge(exp_done, NCH * t + last_chunk[kb] + 3)
                if kb == 0:
                    pe.wait_ge(v_set, t + 1)
                    pe.wait_ge(out_moved, t + 1)
                at = kb % RING * QT
                for quarter in range(4):
                    last = nc.tensor.matmul(out_ps[quarter * D:(quarter + 1) * D, 0:QUARTER], v_now[:, kb * D:(kb + 1) * D],
                                            probs[:, at + quarter * QUARTER:at + (quarter + 1) * QUARTER],
                                            start=kb == 0, stop=kb == KB - 1)
                if kb not in SUM_KB:
                    last.then_inc(pv_done, 1)

            def block_sum(t, kb):
                if kb == SUM_KB[0]:
                    pe.wait_ge(sum_moved, t + 1)
                at = kb % RING * QT
                for quarter in range(4):
                    last = nc.tensor.matmul(sum_ps[quarter * D:(quarter + 1) * D, 0:QUARTER], ones[:, :],
                                            probs[:, at + quarter * QUARTER:at + (quarter + 1) * QUARTER],
                                            start=kb == SUM_KB[0], stop=False)
                last.then_inc(pv_done, 1)

            def fold(t):
                pe.wait_ge(adds_done, ADDS * (t + 2))
                for quarter in range(4):
                    last = nc.tensor.matmul(sum_ps[quarter * D:(quarter + 1) * D, 0:QUARTER], ones[:, :],
                                            prob_sum[:, quarter * QUARTER:(quarter + 1) * QUARTER], start=False, stop=True)
                last.then_inc(fold_done, 1)

            def attend(t, ahead, first=False):
                pe.wait_ge(m_in, 16 * (t + 1))
                due = [j + sum(j >= at for at in INVERT_AT) for j in range(MAXU)]
                done, unit = 0, 0

                def passed(length):
                    nonlocal done, unit
                    done += length
                    while ahead and unit < MAXU and due[unit] * TILE_LEN < done * (MAXU + PIECES):
                        max_unit(t + 2, unit)
                        unit += 1

                def use(t, kb):
                    pv(t, kb)
                    passed(PV_LEN)
                    if kb in SUM_KB:
                        block_sum(t, kb)
                        passed(PV_LEN)

                pv_at = 0
                for k in range(NCH):
                    qk_chunk(t, k)
                    passed(CHUNK_UNITS[k] * QK_LEN)
                    for kb, at in zip(range(LATE_KB, KB), LATE_AT):
                        if k == at and not first:
                            use(t - 1, kb)
                    if k == FOLD_AT and not first:
                        fold(t - 1)
                        passed(PV_LEN)
                    while pv_at < LATE_KB and last_chunk[pv_at] <= k - PV_LAG:
                        use(t, pv_at)
                        pv_at += 1
                for kb in range(pv_at, LATE_KB):
                    use(t, kb)
                for j in range(unit, MAXU if ahead else 0):
                    max_unit(t + 2, j)

            pe.wait_ge(consts_set, 2)
            with pe.Fori(0, 2) as t:
                pe.wait_ge(kv_in, 64)
                pe.wait_ge(q_in, 48 * (t + 1))
                for j in range(MAXU):
                    max_unit(t, j)
            pe.wait_ge(q_in, 48 * 3)
            attend(0, True, first=True)
            with pe.Fori(1, TILES - 2) as t:
                pe.wait_ge(q_in, 48 * (t + 3))
                pe.wait_ge(kv_in, 64 * ((t + 2) // CHUNKS + 1))
                attend(t, True)
            with pe.Fori(TILES - 2, TILES) as t:
                attend(t, False)
            for kb in range(LATE_KB, KB):
                pv(TILES - 1, kb)
                if kb in SUM_KB:
                    block_sum(TILES - 1, kb)
            fold(TILES - 1)

        @block.scalar
        def _(act):
            def save_max(t):
                act.wait_ge(m_ready, t + 1)
                dst = m_dram[bass.ds(t, 1)][0]
                for i in range(4):
                    act.dma_start(dst[:, :, i, :], max_split[32 * i:32 * i + QB, :, :]).then_inc(m_saved, 16)

            def load_max(t):
                act.wait_ge(m_saved, 64 * (t + 2))
                src = m_dram[bass.ds(t, 1)][0].rearrange("c s i r -> s c i r")
                act.dma_start(q_ring[3 * D:3 * D + 2, bass.ds(t % 4 * QT, QT)].rearrange("s (c i r) -> s c i r", i=4, r=32),
                              src).then_inc(m_in, 16)

            def move_sums(t):
                act.wait_ge(fold_done, t + 2)
                act.wait_ge(o_ready, t + 1)
                nc.scalar.activation(out_sum[:, 0, :], out_ps[:, 0:QUARTER], ACT.Copy).then_inc(out_moved, 1)
                nc.scalar.activation(out_sum[:, 1, :], sum_ps[:, 0:QUARTER], ACT.Copy).then_inc(sum_moved, 1)

            def set_v(t):
                g = t // CHUNKS
                act.wait_ge(kv_in, 64 * (g + 1))
                act.wait_ge(pv_done, KB * t + RING)
                nc.scalar.activation(v_now[:, :], v_ring[:, bass.ds(g % 2 * KB * D, KB * D)], ACT.Copy).then_inc(v_set, 1)

            def exps(t, ahead, first=False):
                if first:
                    set_v(t)
                for k in range(NCH):
                    lo, hi = CHUNK_START[k] * BANK, (CHUNK_START[k] + CHUNK_UNITS[k]) * BANK
                    for kb in range(KB):
                        if lo <= kb * QT < hi:
                            act.wait_ge(pv_done, KB * t + kb + 1)
                            old = (kb - RING) % KB
                            if old in added:
                                act.wait_ge(adds_done, ADDS * (t + (kb >= RING)) + added[old])
                    act.wait_ge(qk_done, NCH * t + k + 1)
                    at = lo % (RING * QT)
                    nc.scalar.activation(probs[:, at:at + hi - lo],
                                         score_ps[:, k % 2 * 2:k % 2 * 2 + CHUNK_UNITS[k], :].rearrange("p a b -> p (a b)"),
                                         ACT.Exp, scale=SCALE).then_inc(exp_done, 1)
                    if k == 2 and not first:
                        set_v(t)
                    if k == MOVE_AT and not first:
                        move_sums(t - 1)
                    if ahead and k == 5:
                        save_max(t + 1)
                    if ahead and k == 14:
                        load_max(t + 1)

            act.sem_inc(exp_done, 2)
            act.sem_inc(pv_done, RING)
            act.sem_inc(m_saved, 64)
            act.sem_inc(out_moved, 1)
            act.sem_inc(sum_moved, 1)
            act.sem_inc(o_ready, 1)
            save_max(0)
            load_max(0)
            exps(0, True, first=True)
            with act.Fori(1, TILES - 1) as t:
                exps(t, True)
            exps(TILES - 1, False)
            move_sums(TILES - 1)

        @block.gpsimd
        def _(pool):
            nc.gpsimd.memset(ones[:, :], 1.0).then_inc(consts_set, 1)
            pool.wait_ge(consts_set, 1)
            nc.gpsimd.memset(k_ring[3 * D:3 * D + 2, :], STEP).then_inc(consts_set, 1)
            pool.sem_inc(adds_done, ADDS)

            def add_probs(t):
                for n in range(1, ADDS + 1):
                    kb = POOL_KB[n]
                    pool.wait_ge(exp_done, NCH * t + last_chunk[kb] + 3)
                    if n == 1:
                        pool.wait_ge(fold_done, t + 1)
                    else:
                        pool.wait_ge(adds_done, ADDS * (t + 1) + n - 1)
                    first = probs[:, POOL_KB[0] % RING * QT:POOL_KB[0] % RING * QT + QT] if n == 1 else prob_sum[:, :]
                    nc.gpsimd.tensor_tensor(prob_sum[:, :], first, probs[:, kb % RING * QT:kb % RING * QT + QT],
                                            ALU.add).then_inc(adds_done, 1)
                    if n == NORMALISE_AT and not (isinstance(t, int) and t == 0):
                        normalise(t - 1)

            def normalise(t):
                pool.wait_ge(out_moved, t + 2)
                pool.wait_ge(recip_done, PIECES * (t + 1))
                pool.wait_ge(o_saved, 64 * (t + 1))
                nc.gpsimd.tensor_tensor(o_norm[:, :], out_sum[:, 0, :], recip[:, :], ALU.mult).then_inc(o_ready, 1)

            pool.sem_inc(fold_done, 1)
            add_probs(0)
            with pool.Fori(1, TILES) as t:
                add_probs(t)
            normalise(TILES - 1)

        @block.vector
        def _(dve):
            def invert(t, piece):
                dve.wait_ge(sum_moved, t + 2)
                dve.wait_ge(o_ready, t + 1)
                part = slice(piece * QUARTER // PIECES, (piece + 1) * QUARTER // PIECES)
                nc.vector.reciprocal(recip[:, part], out_sum[:, 1, part]).then_inc(recip_done, 1)

            def reduce_units(t, invert_too=False):
                for j in range(MAXU):
                    if invert_too and j in INVERT_AT:
                        invert(t - 3, INVERT_AT.index(j))
                    pair, r = j // 9, j % 9
                    dve.wait_ge(maxqk_done, MAXU * t + j + 1)
                    if j == 0:
                        dve.wait_ge(dve_step, 3 * t + 3)
                    if r < 8:
                        nc.vector.tensor_reduce(part_max[:, 2 * pair + r // 4, r % 4:r % 4 + 1], max_ps[:, j % 2, :],
                                                AX.X, ALU.max).then_inc(max_read, 1)
                    else:
                        nc.vector.tensor_reduce(part_max[:, 2 * pair:2 * pair + 2, 4],
                                                max_ps[:, j % 2, :].rearrange("p (a b) -> p a b", a=2),
                                                AX.X, ALU.max).then_inc(max_read, 1)
                dve.wait_ge(max_read, MAXU * (t + 1) + 2)
                nc.vector.tensor_reduce(tile_max[:, 0:QB], part_max[:, :, :], AX.X, ALU.max).then_inc(dve_step, 1)
                dve.wait_ge(dve_step, 3 * t + 4)
                dve.wait_ge(m_saved, 64 * (t + 1))
                nc.vector.transpose(max_rows[:, :], tile_max[:, :]).then_inc(dve_step, 1)
                dve.wait_ge(dve_step, 3 * t + 5)
                nc.vector.tensor_scalar(max_split[:, 0, :], max_rows[:, :], -1.0 / STEP, None, ALU.mult).then_inc(dve_step, 1)
                dve.wait_ge(dve_step, 3 * t + 6)
                nc.vector.scalar_tensor_tensor(max_split[:, 1, :], max_rows[:, :], -1.0 / STEP, max_split[:, 0, :],
                                               ALU.mult, ALU.subtract).then_inc(m_ready, 1)

            nc.vector.memset(tile_max[:, :], 0.0).then_inc(dve_step, 1)
            dve.sem_inc(dve_step, 2)
            dve.sem_inc(max_read, 2)
            with dve.Fori(0, 3) as t:
                reduce_units(t)
            with dve.Fori(3, TILES) as t:
                reduce_units(t, True)
            for t in range(TILES - 3, TILES):
                for piece in range(PIECES):
                    invert(t, piece)


def output_projections(nc, x, win_dram, o_dram, w_hi, w_lo, b_hi, b_lo, x1_dram, x1_stats):
    f32, f16 = mybir.dt.float32, mybir.dt.float16
    ALU, ACT = mybir.AluOpType, mybir.ActivationFunctionType
    BATCH, CHUNKS, HD, TOK = o_dram.shape
    N = BATCH * CHUNKS
    M, LANES, IMW, WN, STAT = 96, 128, 96, 4, 512
    KT = HD // M
    CG = 2 * KT
    WIN = TOK // WN
    WT = WIN // LANES
    YR = 4
    PS = 8
    UNITS = CG * WN
    PIECES = TOK // STAT
    ATT_LOADS = WT * KT + KT

    with ExitStack() as ctx:
        def sb(name, shape, dt=f32):
            return ctx.enter_context(nc.sbuf_tensor(name, shape, dt))

        def sem(name):
            return ctx.enter_context(nc.semaphore(name))

        att = sb("att", [M, 2 * 2 * KT * TOK])
        ah, al = sb("ah", [M, 2 * 2 * KT * TOK], f16), sb("al", [M, 2 * 2 * KT * TOK], f16)
        y = sb("y", [M, YR, WIN])
        xb = sb("xb", [M, 2 * CG * TOK])
        w_stage = sb("pw_stage", [M, 2, KT, HD])
        wh, wl = sb("pwh", [M, 2, KT, HD], f16), sb("pwl", [M, 2, KT, HD], f16)
        bias = sb("bias", [M, CG])
        stats = sb("x1_bn", [M, CG, N * PIECES * 6])
        ps = ctx.enter_context(nc.psum_tensor("proj_ps", [LANES, PS, 512], f32))
        w_in, w_hi_set, w_set = sem("pw_in"), sem("pw_hi_set"), sem("pw_set")
        att_in, x_in, high_done, low_done = sem("att_in"), sem("px_in"), sem("high_done"), sem("low_done")
        unit_done, added, evac, x1_saved, stat_done = sem("p_unit_done"), sem("added"), sem("p_evac"), sem("x1_saved"), sem("x1_stat_done")
        block = ctx.enter_context(nc.Block())

        def slot(buf, s, width, at, n):
            return buf[:, bass.ds(s % 2 * width + at, n)]

        @block.sync
        def _(sp):
            def load_att(s):
                if not isinstance(s, int) or s > 0:
                    sp.wait_ge(att_in, 16 * ATT_LOADS * s)
                b, c = s // CHUNKS, s % CHUNKS
                for kt in range(KT):
                    for wt in range(WT):
                        dst = slot(att, s, 2 * KT * TOK, kt * TOK, TOK).rearrange("p (i w) -> p i w", i=WN)
                        sp.dma_start(dst[:, :, wt * LANES:(wt + 1) * LANES],
                                     win_dram[bass.ds(s * WT + wt + 2, 1)][0, kt].rearrange("p (i w) -> p i w", i=WN)).then_inc(att_in, 16)
                    sp.dma_start(slot(att, s, 2 * KT * TOK, (KT + kt) * TOK, TOK),
                                 o_dram[bass.ds(b, 1), bass.ds(c, 1), kt * M:(kt + 1) * M][0, 0]).then_inc(att_in, 16)

            def load_x(s):
                for g in range(CG):
                    sp.dma_start(slot(xb, s, CG * TOK, g * TOK, TOK),
                                 x[bass.ds(s // CHUNKS, 1), g * M:(g + 1) * M, bass.ds(s % CHUNKS * TOK, TOK)][0]).then_inc(x_in, 16)

            for src, (w, bb) in enumerate(((w_hi, b_hi), (w_lo, b_lo))):
                sp.dma_start(w_stage[:, src, :, :], w.rearrange("(t p) n -> p t n", p=M)).then_inc(w_in, 16)
                for kt in range(KT):
                    sp.dma_start(bias[:, src * KT + kt:src * KT + kt + 1], bb[kt * M:(kt + 1) * M, :]).then_inc(w_in, 16)
            def save(s):
                for g in range(CG):
                    sp.wait_ge(stat_done, PIECES * (CG * s + g + 1))
                    sp.dma_start(x1_dram[bass.ds(s // CHUNKS, 1), g * M:(g + 1) * M, bass.ds(s % CHUNKS * TOK, TOK)][0],
                                 slot(xb, s, CG * TOK, g * TOK, TOK)).then_inc(x1_saved, 16)

            sp.sem_inc(x1_saved, 16 * CG)
            load_att(0)
            load_x(0)
            load_att(1)

            def turn(s, more_att):
                if more_att:
                    sp.wait_ge(low_done, 2 * s + 2)
                    load_att(s + 2)
                sp.wait_ge(x1_saved, 16 * CG * (s + 1))
                sp.wait_ge(x_in, 16 * CG * s + 16 * CG)
                load_x(s + 1)
                save(s)

            with sp.Fori(0, N - 2) as s:
                turn(s, True)
            turn(N - 2, False)
            save(N - 1)
            sp.wait_ge(x1_saved, 16 * CG * (N + 1))

        @block.scalar
        def _(act):
            def high(s, src):
                act.wait_ge(att_in, 16 * ATT_LOADS * (s + 1))
                act.wait_ge(unit_done, UNITS * (s + 1))
                nc.scalar.activation(slot(ah, s, 2 * KT * TOK, src * KT * TOK, KT * TOK),
                                     slot(att, s, 2 * KT * TOK, src * KT * TOK, KT * TOK), ACT.Identity).then_inc(high_done, 1)

            def evacs(s, src):
                for u in range(src * UNITS // 2, (src + 1) * UNITS // 2):
                    act.wait_ge(unit_done, UNITS * (s + 2) + u + 1)
                    act.wait_ge(added, UNITS * s + u + 1)
                    nc.scalar.activation(y[:, u % YR, :], ps[0:M, u % PS, 0:WIN], ACT.Identity, bias=bias[:, u // WN:u // WN + 1],
                                         scale=1 / W_UP).then_inc(evac, 1)

            act.wait_ge(w_in, 16 * (2 + CG))
            nc.scalar.mul(wh[:, :, :, :], w_stage[:, :, :, :], W_UP).then_inc(w_hi_set, 1)
            act.sem_inc(evac, PS)
            high(0, 0)
            high(0, 1)
            with act.Fori(0, N - 1) as s:
                high(s + 1, 0)
                evacs(s, 0)
                high(s + 1, 1)
                evacs(s, 1)
            evacs(N - 1, 0)
            evacs(N - 1, 1)

        @block.gpsimd
        def _(pool):
            with pool.Fori(0, N) as s:
                for src in range(2):
                    pool.wait_ge(high_done, 2 * s + src + 1)
                    at, n = src * KT * TOK, KT * TOK
                    nc.gpsimd.tensor_tensor(slot(al, s, 2 * KT * TOK, at, n), slot(att, s, 2 * KT * TOK, at, n),
                                            slot(ah, s, 2 * KT * TOK, at, n), ALU.subtract).then_inc(low_done, 1)

        @block.tensor
        def _(pe):
            pe.wait_ge(w_set, 1)
            pe.sem_inc(unit_done, 2 * UNITS)
            with pe.Fori(0, N) as s:
                for u in range(UNITS):
                    g, i = u // WN, u % WN
                    src, mt = g // KT, g % KT
                    if u % (UNITS // 2) == 0:
                        pe.wait_ge(high_done, 2 * s + src + 1)
                        pe.wait_ge(low_done, 2 * s + src + 1)
                    pe.wait_ge(evac, UNITS * s + u + 1)
                    terms = [(kt, a, b) for kt in range(KT) for a, b in ((0, 0), (0, 1), (1, 0))]
                    for m, (kt, a, b) in enumerate(terms):
                        last = nc.tensor.matmul(ps[0:M, u % PS, 0:WIN], (wh, wl)[a][:, src, kt, mt * M:(mt + 1) * M],
                                                slot((ah, al)[b], s, 2 * KT * TOK, (src * KT + kt) * TOK + i * WIN, WIN),
                                                start=m == 0, stop=m == len(terms) - 1)
                    last.then_inc(unit_done, 1)

        @block.vector
        def _(dve):
            dve.wait_ge(w_hi_set, 1)
            nc.vector.scalar_tensor_tensor(wl[:, :, :, :].rearrange("p a b c -> p (a b c)"), w_stage[:, :, :, :].rearrange("p a b c -> p (a b c)"),
                                           W_UP, wh[:, :, :, :].rearrange("p a b c -> p (a b c)"), ALU.mult, ALU.subtract).then_inc(w_set, 1)
            dve.sem_inc(added, YR)
            with dve.Fori(0, N) as s:
                dve.wait_ge(x_in, 16 * CG * s + 16 * CG)
                for u in range(UNITS):
                    g, i = u // WN, u % WN
                    dve.wait_ge(evac, UNITS * s + u + 1 + PS)
                    view = slot(xb, s, CG * TOK, g * TOK, TOK).rearrange("p (wy dy wx dx) -> p dy dx wy wx", dy=2, dx=2, wx=IMW // 2)[:, i // 2, i % 2]
                    nc.vector.tensor_tensor(view, y[:, u % YR, :].rearrange("p (wy wx) -> p wy wx", wx=IMW // 2), view, ALU.add).then_inc(added, 1)
                    if i == WN - 1:
                        dve.wait_ge(added, UNITS * s + u + 1 + YR)
                        for k in range(PIECES):
                            out = stats[:, g, :][:, bass.ds((s * PIECES + k) * 6, 6)]
                            nc.vector.bn_stats(out, slot(xb, s, CG * TOK, g * TOK + k * STAT, STAT)).then_inc(stat_done, 1)
            dve.wait_ge(stat_done, N * CG * PIECES)
            for g in range(CG):
                for b in range(BATCH):
                    half = CHUNKS * PIECES * 6
                    nc.vector.bn_aggr(x1_stats[:, g, b, :], stats[:, g, b * half:(b + 1) * half])


def displaced_convolution(nc, x1_dram, to_groups, eye, x1_stats, taps_dram, out):
    f32 = mybir.dt.float32
    ALU, ACT = mybir.AluOpType, mybir.ActivationFunctionType
    EPS = 1e-5
    BATCH, C = x1_dram.shape[0], x1_dram.shape[1]
    S, P = taps_dram.shape[0], taps_dram.shape[2]
    CG, NG = x1_stats.shape[1], to_groups.shape[2]
    CP, CGRP = C // P, C // NG
    CH = 24
    POS, GRP = CH // CP, CH // CGRP
    PER = C // CH
    N = BATCH * PER
    SLOTS = 4
    BC = CP // 2

    with ExitStack() as ctx:
        def sb(name, shape):
            return ctx.enter_context(nc.sbuf_tensor(name, shape, f32))

        def sem(name):
            return ctx.enter_context(nc.semaphore(name))

        xc = sb("xc", [S, SLOTS, CH, S])
        xn = sb("xcn", [S, 2, CH, S])
        mid = sb("mid", [S, 2, CP, S])
        res = sb("res", [S, SLOTS, CH, S])
        taps = sb("taps", [S, 2, P, S])
        conv_norm = sb("conv_norm", [S, 2 * BATCH * NG])
        to_g = sb("to_g96", [S, CG, NG])
        eye_sb = sb("eye_sb", [NG, NG])
        ones = sb("ones_g", [NG, S])
        mean_sq = sb("mean_sq1", [S, CG, BATCH, 2])
        square = sb("square1", [S, CG, BATCH])
        group = sb("group1", [NG, BATCH, 2])
        root, newton = sb("root1", [NG, BATCH]), sb("newton1", [NG, BATCH])
        diag = sb("diag", [NG, BATCH, 2, NG])
        mid_ps = ctx.enter_context(nc.psum_tensor("mid_ps", [128, 2, 2, 512], f32))
        out_ps = ctx.enter_context(nc.psum_tensor("conv_ps", [128, 2, 2, 512], f32))
        c_in, c_norm, first_done, mid_done = sem("c_in"), sem("c_norm"), sem("first_done"), sem("mid_done")
        second_done, res_done, c_out = sem("second_done"), sem("res_done"), sem("c_out")
        const_in, taps_in, step, to_act, from_act = sem("t_in"), sem("taps_in"), sem("t_step"), sem("t_to_act"), sem("t_from_act")
        to_pe, from_pe = sem("t_to_pe"), sem("t_from_pe")
        block = ctx.enter_context(nc.Block())

        def image(t, n):
            return t[bass.ds(n // PER, 1), bass.ds(n % PER * CH, CH)][0].rearrange("c (y x) -> y c x", y=S)

        @block.sync
        def _(sp):
            def load(n, slot):
                if not isinstance(n, int) or n > 0:
                    sp.wait_ge(c_in, 16 * n)
                sp.dma_start(xc[:, slot, :, :], image(x1_dram, n)).then_inc(c_in, 16)

            def store(n, slot):
                sp.wait_ge(res_done, POS * (n + 1) + 2)
                sp.dma_start(image(out, n), res[:, slot, :, :]).then_inc(c_out, 16)

            sp.dma_start(to_g[:, :, :], to_groups).then_inc(const_in, 16)
            sp.dma_start(eye_sb[:, :], eye).then_inc(const_in, 16)
            sp.sem_inc(c_out, 16 * SLOTS)
            load(0, 0)
            sp.dma_start(taps[:, :, :, :], taps_dram).then_inc(taps_in, 16)
            for n in range(1, SLOTS - 1):
                load(n, n)
            with sp.Fori(0, N // SLOTS - 1) as turn:
                n = turn * SLOTS
                for k in range(SLOTS):
                    load(n + k + SLOTS - 1, (k + SLOTS - 1) % SLOTS)
                    store(n + k, k)
            for k in range(SLOTS):
                if k == 0:
                    load(N - 1, SLOTS - 1)
                store(N - SLOTS + k, k)
            sp.wait_ge(c_out, 16 * (N + SLOTS))

        @block.tensor
        def _(pe):
            def first(n, k, j):
                m = POS * k + j
                if j == 0:
                    pe.wait_ge(c_norm, GRP * (n + k + 1))
                pe.wait_ge(mid_done, POS * n + m + 1)
                table = taps[:, :, :, :].rearrange("s a p t -> s (a p t)")[:, bass.ds((P + (n + k) % PER * POS + j) * S, S)]
                for c in range(CP):
                    at = c % BC * S
                    last = nc.tensor.matmul(mid_ps[0:S, m % 2, c // BC, at:at + S], xn[:, k % 2, j * CP + c, :], table, start=True, stop=True)
                last.then_inc(first_done, 1)

            def second(n, k, j):
                m = POS * k + j
                pe.wait_ge(mid_done, POS * n + m + 3)
                pe.wait_ge(res_done, POS * n + m + 1)
                table = taps[:, :, :, :].rearrange("s a p t -> s (a p t)")[:, bass.ds(((n + k) % PER * POS + j) * S, S)]
                for c in range(CP):
                    at = c % BC * S
                    last = nc.tensor.matmul(out_ps[0:S, m % 2, c // BC, at:at + S], mid[:, m % 2, c, :], table, start=True, stop=True)
                last.then_inc(second_done, 1)

            pe.wait_ge(to_pe, 1)
            for g in range(CG):
                last = nc.tensor.matmul(mid_ps[0:NG, 0, 0, 0:2 * BATCH], to_g[:, g, :], mean_sq[:, g, :, :].rearrange("p b k -> p (b k)"),
                                        start=g == 0, stop=g == CG - 1)
            last.then_inc(from_pe, 1)
            pe.wait_ge(to_pe, 2)
            nc.tensor.matmul(mid_ps[0:S, 0, 1, 0:2 * BATCH * NG], ones[:, :], diag[:, :, :, :].rearrange("g b k h -> g (b k h)"),
                             start=True, stop=True).then_inc(from_pe, 1)
            pe.wait_ge(taps_in, 16)
            pe.sem_inc(first_done, POS)
            with pe.Fori(0, N // SLOTS) as turn:
                n = turn * SLOTS
                order = [(k, j) for k in range(SLOTS) for j in range(POS)]
                first(n, *order[0])
                for i, (k, j) in enumerate(order):
                    if i + 1 < len(order):
                        first(n, *order[i + 1])
                    second(n, k, j)

        @block.scalar
        def _(act):
            act.wait_ge(to_act, 1)
            nc.scalar.activation(root[:, :], group[:, :, 1], ACT.Sqrt).then_inc(from_act, 1)
            act.sem_inc(mid_done, 2)
            act.sem_inc(second_done, 2)
            with act.Fori(0, N // SLOTS) as turn:
                n = turn * SLOTS
                for m in range(SLOTS * POS):
                    act.wait_ge(first_done, POS * (n + 1) + m + 1)
                    act.wait_ge(second_done, POS * n + m + 1)
                    nc.scalar.copy(mid[:, m % 2, :, :].rearrange("s (h c) t -> s h (c t)", h=2),
                                   mid_ps[0:S, m % 2, :, 0:BC * S]).then_inc(mid_done, 1)

        @block.vector
        def _(dve):
            def normalise(n, k):
                at = n + k
                dve.wait_ge(c_in, 16 * (at + 1))
                if not isinstance(at, int) or at > 0:
                    dve.wait_ge(first_done, POS * at)
                for g in range(GRP):
                    scale = [conv_norm[:, bass.ds((at // PER * 2 + kk) * NG + at % PER * GRP + g, 1)] for kk in range(2)]
                    nc.vector.tensor_scalar(xn[:, k % 2, g * CGRP:(g + 1) * CGRP, :], xc[:, k % SLOTS, g * CGRP:(g + 1) * CGRP, :],
                                            scale[0], scale[1], ALU.subtract, ALU.mult).then_inc(c_norm, 1)

            def finish(n, k):
                for j in range(POS):
                    m = POS * k + j
                    dve.wait_ge(second_done, POS * n + m + 3)
                    if j == 0:
                        dve.wait_ge(c_out, 16 * (n + k + 1))
                    span = slice(j * CP, (j + 1) * CP)
                    nc.vector.tensor_tensor(res[:, k, span, :].rearrange("s (h c) t -> s h (c t)", h=2), out_ps[0:S, m % 2, :, 0:BC * S],
                                            xc[:, k, span, :].rearrange("s (h c) t -> s h (c t)", h=2), ALU.add).then_inc(res_done, 1)

            v = nc.vector
            count = [0]

            def link(ins):
                count[0] += 1
                ins.then_inc(step, 1)
                dve.wait_ge(step, count[0])

            dve.wait_ge(const_in, 32)
            link(v.memset(ones[:, :], 1.0))
            link(v.tensor_tensor(square[:, :, :], x1_stats[:, :, :, 0], x1_stats[:, :, :, 0], ALU.mult))
            link(v.tensor_copy(mean_sq[:, :, :, 0], x1_stats[:, :, :, 0]))
            v.tensor_tensor(mean_sq[:, :, :, 1], x1_stats[:, :, :, 1], square[:, :, :], ALU.add).then_inc(to_pe, 1)
            dve.wait_ge(from_pe, 1)
            link(v.tensor_copy(group[:, :, :], mid_ps[0:NG, 0, 0, 0:2 * BATCH].rearrange("p (b k) -> p b k", k=2)))
            link(v.tensor_tensor(newton[:, :], group[:, :, 0], group[:, :, 0], ALU.mult))
            link(v.tensor_tensor(group[:, :, 1], group[:, :, 1], newton[:, :], ALU.subtract))
            v.tensor_scalar(group[:, :, 1], group[:, :, 1], EPS, None, ALU.add).then_inc(to_act, 1)
            dve.wait_ge(from_act, 1)
            link(v.reciprocal(root[:, :], root[:, :]))
            link(v.tensor_tensor(newton[:, :], root[:, :], root[:, :], ALU.mult))
            link(v.tensor_tensor(newton[:, :], newton[:, :], group[:, :, 1], ALU.mult))
            link(v.tensor_scalar(newton[:, :], newton[:, :], -0.5, 1.5, ALU.mult, ALU.add))
            link(v.tensor_tensor(group[:, :, 1], root[:, :], newton[:, :], ALU.mult))
            for b in range(BATCH):
                for k in range(2):
                    last = v.tensor_scalar(diag[:, b, k, :], eye_sb[:, :], group[:, b, k:k + 1], None, ALU.mult)
                    if (b, k) != (BATCH - 1, 1):
                        link(last)
            last.then_inc(to_pe, 1)
            dve.wait_ge(from_pe, 2)
            link(v.tensor_copy(conv_norm[:, :], mid_ps[0:S, 0, 1, 0:2 * BATCH * NG]))
            dve.sem_inc(res_done, 2)
            normalise(0, 0)
            with dve.Fori(0, N // SLOTS - 1) as turn:
                n = turn * SLOTS
                for k in range(SLOTS):
                    normalise(n, k + 1)
                    finish(n, k)
            for k in range(SLOTS):
                if k + 1 < SLOTS:
                    normalise(N - SLOTS, k + 1)
                finish(N - SLOTS, k)


def displaced_attention_kernel(nc, x, w_hi_qkv, w_hi_proj, b_hi_proj, w_lo_q, w_lo_kv, w_lo_proj, b_lo_proj, offset,
                               to_groups, from_groups, to_groups96, identity, difference, out):
    f32, f16 = mybir.dt.float32, mybir.dt.float16
    BATCH, C, PIX = x.shape
    H, D, CHUNKS, SIZE = 6, 32, 6, 96
    TOK, KEYS = PIX // CHUNKS, PIX // 4
    NG, P = to_groups.shape[2], offset.shape[0]
    WTILES = BATCH * KEYS // 128

    def scratch(name, shape, dt):
        return nc.dram_tensor(name, shape, dt, kind="Internal").ap()

    q_dram = scratch("q_parts", [BATCH, CHUNKS, 2, H, D, TOK], f16)
    k_dram = scratch("k_parts", [BATCH, 2, H, D, KEYS], f16)
    v_dram = scratch("v_rows", [BATCH, H, 128, KEYS // 128 * D], f32)
    m_dram = scratch("maxima", [BATCH * H * CHUNKS, TOK // 128, 2, 4, 32], f16)
    o_dram = scratch("global_out", [BATCH, CHUNKS, H * D, TOK], f32)
    win_dram = scratch("window_out", [WTILES + 2, 2, 96, 512], f32)
    x1_dram = scratch("x1", [BATCH, C, PIX], f32)
    taps_dram = scratch("taps_stored", [SIZE, 2, P, SIZE], f32)

    with ExitStack() as ctx:
        mean_rstd = ctx.enter_context(nc.sbuf_tensor("mean_rstd", [128, C // 128, BATCH, 2], f32))
        x1_stats = ctx.enter_context(nc.sbuf_tensor("x1_stats", [96, C // 96, BATCH, 2], f32))
        with ExitStack() as projections:
            wh, wl = (projections.enter_context(nc.sbuf_tensor(name, [128, C // 128, 6 * H * D], f16)) for name in ("wh", "wl"))
            group_scales_and_tables(nc, x, to_groups, from_groups, mean_rstd, offset, difference, taps_dram,
                                    (w_hi_qkv, w_lo_q, w_lo_kv), wh, wl)
            project_and_window_attention(nc, x, wh, wl, identity, mean_rstd, q_dram, k_dram, v_dram, win_dram)
        global_attention(nc, q_dram, k_dram, v_dram, m_dram, o_dram)
        output_projections(nc, x, win_dram, o_dram, w_hi_proj, w_lo_proj, b_hi_proj, b_lo_proj, x1_dram, x1_stats)
        displaced_convolution(nc, x1_dram, to_groups96, identity[0:NG, 0:NG], x1_stats, taps_dram, out)


def kernel(x, L0_conv_Wh_qkv, L0_conv_Wh_proj, L0_conv_bh_proj, L0_conv_Wl_q, L0_conv_Wl_kv, L0_conv_Wl_proj,
           L0_conv_bl_proj, L1_conv_offset):
    import numpy as np
    import concourse.bacc as bacc
    from concourse.bass_utils import run_bass_kernel_spmd

    x = np.ascontiguousarray(x)
    B, C, HH, WW = x.shape
    G = 32
    channel = np.arange(C)
    member = (channel[:, None] // (C // G) == np.arange(G)[None, :]).astype(np.float32)
    arrays = {
        "x": x.reshape(B, C, HH * WW),
        "w_hi_qkv": L0_conv_Wh_qkv, "w_hi_proj": L0_conv_Wh_proj, "b_hi_proj": L0_conv_bh_proj.reshape(-1, 1),
        "w_lo_q": L0_conv_Wl_q, "w_lo_kv": L0_conv_Wl_kv, "w_lo_proj": L0_conv_Wl_proj, "b_lo_proj": L0_conv_bl_proj.reshape(-1, 1),
        "offset": L1_conv_offset,
        "to_groups": (member * np.float32(G / C)).reshape(C // 128, 128, G).transpose(1, 0, 2),
        "from_groups": member.T,
        "to_groups96": (member * np.float32(G / C)).reshape(C // 96, 96, G).transpose(1, 0, 2),
        "identity": np.eye(128, dtype=np.float32),
        "difference": (np.arange(HH)[:, None] - np.arange(HH)[None, :]).astype(np.float32),
    }
    arrays = {name: np.ascontiguousarray(a) for name, a in arrays.items()}
    nc = bacc.Bacc("TRN2", target_bir_lowering=False, num_devices=1)
    args = [nc.dram_tensor(name, list(a.shape), mybir.dt.from_np(a.dtype), kind="ExternalInput").ap() for name, a in arrays.items()]
    out = nc.dram_tensor("out", [B, C, HH * WW], mybir.dt.float32, kind="ExternalOutput").ap()
    displaced_attention_kernel(nc, *args, out)
    result = run_bass_kernel_spmd(nc, [arrays], core_ids=[0]).results[0]["out"]
    return result.reshape(B, C, HH, WW)
```
